# Optimizing a Trainium2 kernel written in Bass

```python
import numpy as np
import jax
import jax.numpy as jnp

def _softmax(x, axis=-1):
    return jax.nn.softmax(x, axis=axis)

def _gelu(x):
    return jax.nn.gelu(x, approximate=True)

def _silu(x):
    return jax.nn.silu(x)

def _sigmoid(x):
    return jax.nn.sigmoid(x)

def _layernorm(x, axis=-1, eps=1e-05):
    m = jnp.mean(x, axis=axis, keepdims=True)
    v = jnp.var(x, axis=axis, keepdims=True)
    return (x - m) / jnp.sqrt(v + eps)

def _scatter_add(tgt, idx, src, axis=0):
    return tgt.at[idx].add(src)

def _segment_sum(src, seg, n):
    return jax.ops.segment_sum(src, seg, n)
kernel_name = 'mk_adj_ffn_d1_adj_r2_2752d1'

def setup_inputs(seed: int=0):
    np.random.seed(seed)
    _w = jnp.asarray

    def _rec_inputs():
        import jax
        import jax.numpy as jnp
        _gk = jax.random.key(seed)
        x = -0.0005207 + 1.001 * jax.random.normal(jax.random.fold_in(_gk, 1), (8, 1024, 128), jnp.float32)
        _a = jax.random.bernoulli(jax.random.fold_in(_gk, 2), 0.00390625, (1024, 1024))
        adj = _a.astype(jnp.int32)
        return (x, adj)
    x, adj = _rec_inputs()

    def _L0_gnn_setup():
        import jax, jax.numpy as jnp
        import numpy as np
        import math
        CHUNK = 128
        NUM_HEADS = 4
        EPS = 1e-05
        key = jax.random.key(seed)
        ks = jax.random.split(key, 12)
        B, N, F = (4, 1024, 128)
        x = jax.random.normal(ks[0], (B, N, F), dtype=jnp.float32)
        adj_matrix = jax.random.randint(ks[1], (N, N), 0, 2, dtype=jnp.int32)
        s = 1.0 / math.sqrt(F)
        Wq = jax.random.normal(ks[2], (F, F), dtype=jnp.float32) * s
        bq = jnp.zeros((F,), dtype=jnp.float32)
        Wk = jax.random.normal(ks[3], (F, F), dtype=jnp.float32) * s
        bk = jnp.zeros((F,), dtype=jnp.float32)
        Wv = jax.random.normal(ks[4], (F, F), dtype=jnp.float32) * s
        bv = jnp.zeros((F,), dtype=jnp.float32)
        Wo = jax.random.normal(ks[5], (F, F), dtype=jnp.float32) * s
        bo = jnp.zeros((F,), dtype=jnp.float32)
        gamma = jnp.ones((F,), dtype=jnp.float32)
        beta = jnp.zeros((F,), dtype=jnp.float32)
        return {'x': x, 'adj_matrix': adj_matrix, 'Wq': Wq, 'bq': bq, 'Wk': Wk, 'bk': bk, 'Wv': Wv, 'bv': bv, 'Wo': Wo, 'bo': bo, 'gamma': gamma, 'beta': beta}
    _L0_gnn_all = _L0_gnn_setup()
    _L0_gnn_in = {k: v for k, v in _L0_gnn_all.items() if k in ('Wq', 'bq', 'Wk', 'bk', 'Wv', 'bv', 'Wo', 'bo', 'gamma', 'beta')}
    del _L0_gnn_all

    def _L0_ffn_setup():
        import jax, jax.numpy as jnp
        import numpy as np
        TOP_K = 2
        key = jax.random.key(seed)
        ks = jax.random.split(key, 4)
        B, L, D, H, E = (8, 2048, 128, 512, 8)
        s = 0.02
        return {'x': jax.random.normal(ks[0], (B, L, D), jnp.float32), 'Wg': jax.random.normal(ks[1], (D, E), jnp.float32) * s, 'bg': jnp.zeros((E,), jnp.float32), 'W1': jax.random.normal(ks[2], (E, D, H), jnp.float32) * s, 'b1': jnp.zeros((E, H), jnp.float32), 'W2': jax.random.normal(ks[3], (E, H, D), jnp.float32) * s, 'b2': jnp.zeros((E, D), jnp.float32)}
    _L0_ffn_all = _L0_ffn_setup()
    _L0_ffn_in = {k: v for k, v in _L0_ffn_all.items() if k in ('Wg', 'bg', 'W1', 'b1', 'W2', 'b2')}
    del _L0_ffn_all
    return {'x': x, 'adj': adj, 'L0_gnn_Wq': _L0_gnn_in['Wq'], 'L0_gnn_bq': _L0_gnn_in['bq'], 'L0_gnn_Wk': _L0_gnn_in['Wk'], 'L0_gnn_bk': _L0_gnn_in['bk'], 'L0_gnn_Wv': _L0_gnn_in['Wv'], 'L0_gnn_bv': _L0_gnn_in['bv'], 'L0_gnn_Wo': _L0_gnn_in['Wo'], 'L0_gnn_bo': _L0_gnn_in['bo'], 'L0_gnn_gamma': _L0_gnn_in['gamma'], 'L0_gnn_beta': _L0_gnn_in['beta'], 'L0_ffn_Wg': _L0_ffn_in['Wg'], 'L0_ffn_bg': _L0_ffn_in['bg'], 'L0_ffn_W1': _L0_ffn_in['W1'], 'L0_ffn_b1': _L0_ffn_in['b1'], 'L0_ffn_W2': _L0_ffn_in['W2'], 'L0_ffn_b2': _L0_ffn_in['b2']}

def reference(x, adj, L0_gnn_Wq, L0_gnn_bq, L0_gnn_Wk, L0_gnn_bk, L0_gnn_Wv, L0_gnn_bv, L0_gnn_Wo, L0_gnn_bo, L0_gnn_gamma, L0_gnn_beta, L0_ffn_Wg, L0_ffn_bg, L0_ffn_W1, L0_ffn_b1, L0_ffn_W2, L0_ffn_b2):
    import jax
    import jax.numpy as jnp

    def _L0_gnn_ref(x, adj_matrix, Wq, bq, Wk, bk, Wv, bv, Wo, bo, gamma, beta):
        import jax, jax.numpy as jnp
        import numpy as np
        import math
        CHUNK = 128
        NUM_HEADS = 4
        EPS = 1e-05
        B, N, Fin = x.shape
        H = NUM_HEADS
        Dout = Wq.shape[0]
        Dh = Dout // H
        Nc = N // CHUNK
        q = (x @ Wq.T + bq).reshape(B, N, H, Dh).transpose(0, 2, 1, 3)
        k = (x @ Wk.T + bk).reshape(B, N, H, Dh).transpose(0, 2, 1, 3)
        v = (x @ Wv.T + bv).reshape(B, N, H, Dh).transpose(0, 2, 1, 3)
        kc = k.reshape(B, H, Nc, CHUNK, Dh)
        vc = v.reshape(B, H, Nc, CHUNK, Dh)
        scores = jnp.einsum('bhnd,bhjcd->bhnjc', q, kc) / jnp.sqrt(jnp.asarray(Dh, dtype=q.dtype))
        scores = jnp.clip(scores, -10.0, 10.0)
        mask = adj_matrix.reshape(N, Nc, CHUNK)[None, None]
        scores = jnp.where(mask == 0, jnp.asarray(-10.0, scores.dtype), scores)
        attn = jax.nn.softmax(scores, axis=-1)
        ctx = jnp.einsum('bhnjc,bhjcd->bhnd', attn, vc)
        ctx = ctx.transpose(0, 2, 1, 3).reshape(B, N, Dout)
        out = ctx @ Wo.T + bo
        out = out + x
        mu = jnp.mean(out, axis=-1, keepdims=True)
        var = jnp.mean(jnp.square(out - mu), axis=-1, keepdims=True)
        out = (out - mu) * jax.lax.rsqrt(var + EPS) * gamma + beta
        return out

    def _L0_ffn_ref(x, Wg, bg, W1, b1, W2, b2):
        import jax, jax.numpy as jnp
        import numpy as np
        TOP_K = 2
        B, L, D = x.shape
        E = W1.shape[0]
        xf = x.reshape(-1, D)
        gate_logits = xf @ Wg + bg
        top_w, top_i = jax.lax.top_k(gate_logits, TOP_K)
        top_w = jax.nn.softmax(top_w, axis=-1)
        w_dense = jnp.sum(jax.nn.one_hot(top_i, E, dtype=xf.dtype) * top_w[..., None], axis=1)
        out = jnp.zeros_like(xf)
        for e in range(E):
            h = jax.nn.gelu(xf @ W1[e] + b1[e], approximate=False)
            out = out + w_dense[:, e:e + 1] * (h @ W2[e] + b2[e])
        return out.reshape(B, L, D)
    x = x + _L0_gnn_ref(_layernorm(x, axis=-1), adj, L0_gnn_Wq, L0_gnn_bq, L0_gnn_Wk, L0_gnn_bk, L0_gnn_Wv, L0_gnn_bv, L0_gnn_Wo, L0_gnn_bo, L0_gnn_gamma, L0_gnn_beta)
    x = x + _L0_ffn_ref(_layernorm(x, axis=-1), L0_ffn_Wg, L0_ffn_bg, L0_ffn_W1, L0_ffn_b1, L0_ffn_W2, L0_ffn_b2)
    return x

_drawn_inputs = setup_inputs


def setup_inputs(seed=0):
    import zlib

    import numpy as np

    out = dict(_drawn_inputs(seed))
    spreads = {'L0_gnn_bq': (0.0, 0.8),
     'L0_gnn_bk': (0.0, 2.0),
     'L0_gnn_bv': (0.0, 0.1),
     'L0_gnn_bo': (0.0, 0.279),
     'L0_gnn_gamma': (1.0, 0.2),
     'L0_gnn_beta': (0.0, 0.1),
     'L0_ffn_bg': (0.0, 0.313),
     'L0_ffn_b1': (0.0, 0.8),
     'L0_ffn_b2': (0.0, 0.1)}
    factors = {}
    for name, (base, spread) in spreads.items():
        noise = np.random.default_rng([zlib.crc32(name.encode()), seed]).standard_normal(out[name].shape)
        drawn = base * np.exp(spread * noise) if base else spread * noise
        out[name] = jnp.asarray(drawn.astype(out[name].dtype))
    for name, factor in factors.items():
        out[name] = (out[name] * factor).astype(out[name].dtype)
    return out
```

```python
from contextlib import ExitStack

import concourse.bass as bass
from concourse import mybir

F32 = mybir.dt.float32
F32R = mybir.dt.float32r
BF16 = mybir.dt.bfloat16
I32 = mybir.dt.int32
U32 = mybir.dt.uint32
ALU = mybir.AluOpType
ACT = mybir.ActivationFunctionType

P = 128
B, N, D = 8, 1024, 128
H, DH = 4, 32
NC = N // P
T = N // P
NQ = 512
UNITS = (N // NQ) * NC
SLOTS = 2 * UNITS
EX, HID = 8, 512
HB = HID // P
SCALE = float(DH) ** -0.5
CLIP = 10.0
EPS = 1e-5
RING = 4
Q_PARTS = (0, 1, 0, 1)
K_PARTS = (0, 0, 1, 1)
PIECES = {2: ("xT", 0), 3: ("xT", 1), 4: ("wo", 0), 5: ("wo", 1), 6: ("q", 0), 7: ("q", 1),
          8: ("k", 0), 9: ("k", 1), 10: ("v", 0), 11: ("v", 1), 12: ("yT", 0), 13: ("yT", 1),
          14: ("gate", 0)}
NEXT = ("xT", "q", "k", "v")


def attention_phase(nc, a, yT_dram, x2_dram, wd_all):
    with ExitStack() as ctx:
        def sb(name, shape, dt=F32):
            return ctx.enter_context(nc.sbuf_tensor(name, shape, dt))

        def pb(name, shape, dt=F32):
            return ctx.enter_context(nc.psum_tensor(name, shape, dt))

        def sem(name):
            return ctx.enter_context(nc.semaphore(name))

        w_q, w_k, w_v, w_o = (sb(n, [P, D]) for n in ("w_q", "w_k", "w_v", "w_o"))
        ident = sb("ident", [P, P])
        w_g = sb("w_g", [P, EX])
        b_q, b_k = sb("b_q", [P, 1]), sb("b_k", [P, 1])
        b_v, b_o, gamma, beta = (sb(n, [P, D]) for n in ("b_v", "b_o", "gamma", "beta"))
        b_g, iota_e = sb("b_g", [P, EX]), sb("iota_e", [P, EX])
        ones = sb("ones", [P, DH])
        minus_half = sb("minus_half", [P, T])
        cap = sb("cap", [P, NC, N], BF16)
        q_stack = [sb(f"q_stack{i}", [P, H, N], F32R) for i in range(2)]
        k_stack = [sb(f"k_stack{i}", [P, H, N], F32R) for i in range(2)]
        v_sb = [sb(f"v_sb{i}", [P, NC, D]) for i in range(2)]
        ctxT = [sb(f"ctxT{i}", [P, N]) for i in range(2)]
        xn_bo = [sb(f"xn_bo{i}", [P, T, D]) for i in range(2)]
        x_in, xn, x_res = sb("x_in", [P, T, D]), sb("xn", [P, T, D]), sb("x_res", [P, T, D])
        xnT = sb("xnT", [P, N])
        q_part = [sb(f"q_part{i}", [P, N], F32R) for i in range(2)]
        k_part = [sb(f"k_part{i}", [P, N], F32R) for i in range(2)]
        full = sb("full", [P, 2, NQ])
        g, yn, ynT = sb("g", [P, T, D]), sb("yn", [P, T, D]), sb("ynT", [P, N])
        st_x, st_g, st_y = (sb(n, [P, T, 6]) for n in ("st_x", "st_g", "st_y"))
        mv_x, mv_g, mv_y = (sb(n, [P, T, 2]) for n in ("mv_x", "mv_g", "mv_y"))
        rs_x, rs_g, rs_y = (sb(n, [P, T]) for n in ("rs_x", "rs_g", "rs_y"))
        logit, top, topi = sb("logit", [P, T, EX]), sb("top", [P, T, 8]), sb("topi", [P, T, 8], U32)
        topf = sb("topf", [P, T, 2])
        wgt, gap, egap = sb("wgt", [P, T, 2]), sb("gap", [P, T]), sb("egap", [P, T])
        hot = sb("hot", [P, 2, T, EX])
        probs = sb("probs", [P, RING, H, NQ])
        ln_den, recip, prod = sb("ln_den", [P, 2, NQ]), sb("recip", [P, 2, NQ]), sb("prod", [P, 2, NQ])

        ps_s = [pb(f"ps_s{i}", [P, 2, NQ]) for i in range(2)]
        ps_c = [pb(f"ps_c{i}", [P, NQ]) for i in range(2)]
        ps_d = pb("ps_d", [P, NQ])
        ps_x = pb("ps_x", [P, NQ])

        const_in = sem("const_in")
        adj_in = [sem(f"adj_in{i}") for i in range(2)]
        adj_hot, adj_read = sem("adj_hot"), sem("adj_read")
        cap_ready, ones_ready = sem("cap_ready"), sem("ones_ready")
        bias_ready = sem("bias_ready")
        x_loaded, res_loaded = sem("x_loaded"), sem("res_loaded")
        stats_x, rstd_x, xn_ready, xnbo_ready = sem("stats_x"), sem("rstd_x"), sem("xn_ready"), sem("xnbo_ready")
        xT_ready, xT_taken = sem("xT_ready"), sem("xT_taken")
        qk_ready, qk_taken, qk_high, qk_low = sem("qk_ready"), sem("qk_taken"), sem("qk_high"), sem("qk_low")
        v_ready, v_taken = sem("v_ready"), sem("v_taken")
        stacked = [sem(f"stacked{i}") for i in range(2)]
        scores_ready, clipped, probs_ready = sem("scores_ready"), sem("clipped"), sem("probs_ready")
        ctx_ready, den_ready = sem("ctx_ready"), sem("den_ready")
        lnden_ready, recip_ready, scaled, summed = sem("lnden_ready"), sem("recip_ready"), sem("scaled"), sem("summed")
        wo_ready, wo_taken = sem("wo_ready"), sem("wo_taken")
        stats_g, rstd_g, tn_ready, x2_ready = sem("stats_g"), sem("rstd_g"), sem("tn_ready"), sem("x2_ready")
        stats_y, rstd_y, yn_ready = sem("stats_y"), sem("rstd_y"), sem("yn_ready")
        yT_ready, yT_taken, gate_ready, gate_taken = sem("yT_ready"), sem("yT_taken"), sem("gate_ready"), sem("gate_taken")
        gap_ready, egap_ready, weights_ready = sem("gap_ready"), sem("egap_ready"), sem("weights_ready")
        x2_stored, yT_stored = sem("x2_stored"), sem("yT_stored")
        dve_step, pool_step = sem("dve_step"), sem("pool_step")

        x_v = a["x"].rearrange("b (t p) d -> b p t d", p=P)
        x2_v = x2_dram.rearrange("(b t p) d -> b p t d", p=P, t=T)
        yT_v = yT_dram.rearrange("p (b n) -> b p n", b=B)
        adj_v = a["adjT"].rearrange("(j p) n -> j p n", p=P)
        adj_buf = [g[:, :, :].bitcast(I32), yn[:, :, :].bitcast(I32)]
        hot_buf = [x_res[:, :, :], ynT[:, :].rearrange("p (t d) -> p t d", t=T)]

        def wait_apart(eng, s, count):
            if not isinstance(count, int):
                count = eng.snap(count)
                eng.compute_val(count)
            eng.wait_ge(const_in, 14 * 16)
            eng.wait_ge(s, count)

        def before(b, s, lag):
            return (b, s - lag) if s >= lag else (b - 1, s - lag + UNITS)

        def bodies(eng, body):
            body(0, 0, first=True)
            with eng.Fori(0, (B - 2) // 2) as i:
                body(2 * i + 1, 1)
                body(2 * i + 2, 0)
            body(B - 1, 1, last=True)

        block = ctx.enter_context(nc.Block())

        @block.sync
        def _(sp):
            consts = [(ident, "ident"), (w_q, "WqT"), (w_k, "WkT"), (w_v, "WvT"), (w_o, "WoT"), (w_g, "Wg"),
                      (b_q, "bq"), (b_k, "bk"), (b_v, "bv"), (b_o, "bo"), (gamma, "gamma"), (beta, "beta"),
                      (b_g, "bg"), (iota_e, "iota")]

            def load_x(b):
                sp.dma_start(x_in[:, :, :], x_v[b]).then_inc(x_loaded, 16)

            def load_res(b):
                sp.dma_start(x_res[:, :, :], x_v[b]).then_inc(res_loaded, 16)

            def load_adj(j):
                if j >= 2:
                    sp.wait_ge(adj_hot, j - 1)
                sp.dma_start(adj_buf[j % 2], adj_v[j].rearrange("p (t d) -> p t d", t=T)).then_inc(adj_in[j % 2], 16)

            def stack(par, which, b):
                stacks, parts, order = ((q_stack, q_part, Q_PARTS), (k_stack, k_part, K_PARTS))[which]
                sp.wait_ge(qk_high, 4 * b + 2 * which + 2)
                sp.wait_ge(qk_low, 4 * b + 2 * which + 2)
                for row, part in enumerate(order):
                    for h in range(H):
                        sp.dma_start(stacks[par][DH * row:DH * (row + 1), h, :].bitcast(F32),
                                     parts[part][DH * h:DH * (h + 1), :].bitcast(F32)).then_inc(stacked[par], 16)

            load_x(0)
            for dst, name in consts:
                sp.dma_start(dst[:, :], a[name]).then_inc(const_in, 16)
            load_adj(0)
            load_adj(1)
            sp.wait_ge(xn_ready, 1)
            load_x(1)
            stack(0, 0, 0)
            stack(0, 1, 0)
            for j in range(2, NC):
                load_adj(j)
            sp.wait_ge(cap_ready, NC)
            load_res(0)

            def body(b, par, first=False, last=False):
                if not last:
                    if not first:
                        sp.wait_ge(scores_ready, SLOTS * b)
                    stack(1 - par, 0, b + 1)
                    stack(1 - par, 1, b + 1)
                if not first:
                    store(b - 1)
                    load_res(b)

            def store(b):
                sp.wait_ge(x2_ready, b + 1)
                sp.dma_start(x2_v[b], g[:, :, :]).then_inc(x2_stored, 16)
                sp.wait_ge(yT_taken, 2 * b + 2)
                sp.dma_start(yT_v[b], ynT[:, :]).then_inc(yT_stored, 16)

            def loading(b, par, first=False, last=False):
                if not last:
                    sp.wait_ge(xn_ready, b + 2)
                    if not first or True:
                        pass

            def whole(b, par, first=False, last=False, ahead=True):
                if ahead:
                    sp.wait_ge(xn_ready, b + 2)
                    load_x(b + 2)
                body(b, par, first, last)

            whole(0, 0, first=True)
            with sp.Fori(0, (B - 4) // 2) as i:
                whole(2 * i + 1, 1)
                whole(2 * i + 2, 0)
            whole(B - 3, 1)
            whole(B - 2, 0, ahead=False)
            body(B - 1, 1, last=True)
            store(B - 1)
            sp.wait_ge(x2_stored, 16 * B)
            sp.wait_ge(yT_stored, 16 * B)

        @block.tensor
        def _(pe):
            def spare_free(b, s, first, last):
                if s > min(PIECES):
                    order = [k for k in sorted(PIECES) if k < s and piece_runs(PIECES[k][0], first, last)]
                    if order:
                        kind, half = PIECES[order[-1]]
                        taken(kind, half, b)
                        return
                pe.wait_ge(v_taken, 2 * b + 2)

            def taken(kind, half, b):
                sem_, count = {"xT": (xT_taken, 2 * (b + 1)), "wo": (wo_taken, 2 * (b - 1)),
                               "q": (qk_taken, 4 * (b + 1)), "k": (qk_taken, 4 * (b + 1) + 2),
                               "v": (v_taken, 2 * (b + 1)), "yT": (yT_taken, 2 * (b - 1)),
                               "gate": (gate_taken, b - 1)}[kind]
                pe.wait_ge(sem_, count + half + 1)

            def piece(kind, half, b):
                lo = half * NQ
                if kind == "xT":
                    pe.wait_ge(xn_ready, b + 1)
                    for t in range(4):
                        last = pe.transpose(ps_x[:, t * P:(t + 1) * P], xn[:, 4 * half + t, :], ident[:, :])
                    last.then_inc(xT_ready, 1)
                elif kind in "qk":
                    pe.wait_ge(xT_taken, 2 * b + half + 1)
                    w = w_q if kind == "q" else w_k
                    pe.matmul(ps_x[:, :], w[:, :], xnT[:, lo:lo + NQ], start=True, stop=True).then_inc(qk_ready, 1)
                elif kind == "v":
                    for t in range(4):
                        last = pe.matmul(ps_x[:, t * P:(t + 1) * P], xnT[:, lo + t * P:lo + (t + 1) * P], w_v[:, :],
                                         start=True, stop=True)
                    last.then_inc(v_ready, 1)
                elif kind == "wo":
                    pe.wait_ge(summed, 14 * b + 7 * (half + 1))
                    src = ctxT_of(b)
                    for t in range(4):
                        last = pe.matmul(ps_x[:, t * P:(t + 1) * P], src[:, lo + t * P:lo + (t + 1) * P], w_o[:, :],
                                         start=True, stop=True)
                    last.then_inc(wo_ready, 1)
                elif kind == "yT":
                    pe.wait_ge(yn_ready, b + 1)
                    for t in range(4):
                        last = pe.transpose(ps_x[:, t * P:(t + 1) * P], yn[:, 4 * half + t, :], ident[:, :])
                    last.then_inc(yT_ready, 1)
                else:
                    pe.wait_ge(yT_taken, 2 * b + 2)
                    for t in range(T):
                        last = pe.matmul(ps_x[:, t * EX:(t + 1) * EX], ynT[:, t * P:(t + 1) * P], w_g[:, :],
                                         start=True, stop=True)
                    last.then_inc(gate_ready, 1)

            par_now = [0]

            def ctxT_of(b):
                return ctxT[par_now[0]]

            def scores(b, par, u, pair):
                half, j = divmod(u, NC)
                slot = 2 * u + pair
                if not (isinstance(b, int) and b == 0 and slot < 2):
                    pe.wait_ge(clipped, SLOTS * b + slot - 1)
                for n in range(2):
                    h = 2 * pair + n
                    last = pe.matmul(ps_s[pair][:, n, :], k_stack[par][:, h, j * P:(j + 1) * P],
                                     q_stack[par][:, h, half * NQ:(half + 1) * NQ], start=True, stop=True)
                last.then_inc(scores_ready, 1)

            def context(b, par, u):
                j = u % NC
                pe.wait_ge(probs_ready, SLOTS * b + 2 * u + 2)
                if not (isinstance(b, int) and b == 0 and u < 2):
                    pe.wait_ge(scaled, UNITS * b + u - 1)
                for h in range(H):
                    last = pe.matmul(ps_c[u % 2][DH * h:DH * (h + 1), :], v_sb[par][:, j, DH * h:DH * (h + 1)],
                                     probs[:, u % RING, h, :], start=True, stop=True, tile_position=(0, DH * h))
                last.then_inc(ctx_ready, 1)

            def denominators(b, u):
                if not (isinstance(b, int) and b == 0 and u < 1):
                    pe.wait_ge(lnden_ready, UNITS * b + u)
                for h in range(H):
                    last = pe.matmul(ps_d[DH * h:DH * (h + 1), :], ones[:, :], probs[:, u % RING, h, :],
                                     start=True, stop=True, tile_position=(0, DH * h))
                last.then_inc(den_ready, 1)

            def body(b, par, first=False, last=False):
                pe.wait_ge(stacked[par], 512 * (half_of(b, par) + 1))
                for s in range(UNITS):
                    if s == 0:
                        pe.wait_ge(v_taken, 2 * b + 2)
                    scores(b, par, s, 0)
                    run = not (first and s < 2)
                    bb, u = before(b, s, 2)
                    if run:
                        context(bb, par if s >= 2 else 1 - par, u)
                    scores(b, par, s, 1)
                    if run:
                        denominators(bb, u)
                    if s in PIECES:
                        kind, half = PIECES[s]
                        if piece_runs(kind, first, last):
                            spare_free(b, s, first, last)
                            par_now[0] = 1 - par
                            piece(kind, half, b + 1 if kind in NEXT else b - 1)

            def half_of(b, par):
                if isinstance(b, int):
                    return b // 2
                return pair_index[0] + (1 if par == 0 else 0)

            pair_index = [None]
            pe.wait_ge(const_in, 14 * 16)
            prev = None
            for kind in ("xT", "q", "k", "v"):
                for half in range(2):
                    if prev is not None:
                        taken(prev[0], prev[1], -1)
                    piece(kind, half, 0)
                    prev = (kind, half)
            pe.wait_ge(ones_ready, 1)
            body(0, 0, first=True)
            with pe.Fori(0, (B - 2) // 2) as i:
                pair_index[0] = i
                body(2 * i + 1, 1)
                body(2 * i + 2, 0)
            body(B - 1, 1, last=True)
            for u in (UNITS - 2, UNITS - 1):
                context(B - 1, 1, u)
                denominators(B - 1, u)
            par_now[0] = 1
            prev = ("gate", 0)
            for kind, half in (("wo", 0), ("wo", 1), ("yT", 0), ("yT", 1), ("gate", 0)):
                taken(prev[0], prev[1], B if prev[0] != "gate" else B - 1)
                piece(kind, half, B - 1)
                prev = (kind, half)

        @block.scalar
        def _(act):
            def probabilities(b, u, pair):
                act.wait_ge(clipped, SLOTS * b + 2 * u + pair + 1)
                buf = probs[:, u % RING, 2 * pair:2 * pair + 2, :]
                act.activation(buf, buf, ACT.Exp).then_inc(probs_ready, 1)

            def log_den(b, u):
                act.wait_ge(den_ready, UNITS * b + u + 1)
                act.activation(ln_den[:, u % 2, :], ps_d[:, :], ACT.Ln).then_inc(lnden_ready, 1)

            def reciprocal(b, u):
                act.wait_ge(lnden_ready, UNITS * b + u + 1)
                if not (isinstance(b, int) and b == 0 and u < 2):
                    act.wait_ge(scaled, UNITS * b + u - 1)
                act.activation(recip[:, u % 2, :], ln_den[:, u % 2, :], ACT.Exp, scale=-1.0).then_inc(recip_ready, 1)

            def take(kind, half, b):
                lo = half * NQ
                if kind == "xT":
                    act.wait_ge(xT_ready, 2 * b + half + 1)
                    act.activation(xnT[:, lo:lo + NQ], ps_x[:, :], ACT.Copy).then_inc(xT_taken, 1)
                elif kind in ("q", "k"):
                    n = 4 * b + 2 * (kind == "k") + half
                    act.wait_ge(qk_ready, n + 1)
                    if not (isinstance(b, int) and b == 0 and kind == "q"):
                        act.wait_ge(qk_low, n - 1)
                    act.activation(full[:, half, :], ps_x[:, :], ACT.Identity, bias=(b_q if kind == "q" else b_k)[:, :],
                                   scale=SCALE if kind == "q" else 1.0).then_inc(qk_taken, 1)
                    act.wait_ge(qk_taken, n + 1)
                    if not (isinstance(b, int) and b == 0):
                        act.wait_ge(stacked_sem(b), stacked_count(b))
                    part = (q_part if kind == "q" else k_part)[0]
                    act.activation(part[:, lo:lo + NQ], full[:, half, :], ACT.Copy).then_inc(qk_high, 1)
                elif kind == "yT":
                    act.wait_ge(yT_ready, 2 * b + half + 1)
                    if not (isinstance(b, int) and b == 0):
                        act.wait_ge(yT_stored, 16 * b)
                    act.activation(ynT[:, lo:lo + NQ], ps_x[:, :], ACT.Copy).then_inc(yT_taken, 1)

            now = [None, None]

            def stacked_sem(b):
                return stacked[now[0]]

            def stacked_count(b):
                return now[1]

            def gap_exp(b):
                act.wait_ge(gap_ready, b + 1)
                act.activation(egap[:, :], gap[:, :], ACT.Exp).then_inc(egap_ready, 1)

            def body(b, par, first=False, last=False):
                for s in range(UNITS):
                    run = not (first and s < 3)
                    bb, u = before(b, s, 3)
                    if run:
                        log_den(bb, u)
                    probabilities(b, s, 0)
                    if run:
                        reciprocal(bb, u)
                    probabilities(b, s, 1)
                    if s - 1 in PIECES:
                        kind, half = PIECES[s - 1]
                        if piece_runs(kind, first, last):
                            now[0], now[1] = par, 512 * (half_of(b, par) + 1)
                            take(kind, half, b + 1 if kind in NEXT else b - 1)
                    if s == UNITS - 1 and not first:
                        gap_exp(b - 1)

            pair_index = [None]

            def half_of(b, par):
                if isinstance(b, int):
                    return b // 2
                return pair_index[0] + (1 if par == 0 else 0)

            act.wait_ge(bias_ready, 1)
            for j in range(NC):
                if j in (2, 4):
                    pass
            for kind in ("xT", "q", "k"):
                for half in range(2):
                    take(kind, half, 0)
            for j in range(NC):
                act.wait_ge(adj_hot, j + 1)
                act.activation(cap[:, j, :].rearrange("p (t d) -> p t d", t=T), hot_buf[j % 2], ACT.Copy,
                               bias=-CLIP, scale=2 * CLIP).then_inc(cap_ready, 1)
            body(0, 0, first=True)
            with act.Fori(0, (B - 2) // 2) as i:
                pair_index[0] = i
                body(2 * i + 1, 1)
                body(2 * i + 2, 0)
            body(B - 1, 1, last=True)
            for u in range(UNITS - 3, UNITS):
                log_den(B - 1, u)
                reciprocal(B - 1, u)
            take("yT", 0, B - 1)
            take("yT", 1, B - 1)
            gap_exp(B - 1)

        @block.vector
        def _(dve):
            chained = [0, 0]

            def step(ins):
                chained[1] += 1
                ins.then_inc(dve_step, 1)
                dve.wait_ge(dve_step, chained[0] + chained[1])

            def plain_step(ins):
                chained[1] += 1
                ins.then_inc(dve_step, 1)
                wait_apart(dve, dve_step, chained[0] + chained[1])

            def clip(b, u, pair):
                half, j = divmod(u, NC)
                dve.wait_ge(scores_ready, SLOTS * b + 2 * u + pair + 1)
                if isinstance(b, int) and b == 0 and half == 0:
                    dve.wait_ge(cap_ready, j + 1)
                if not (isinstance(b, int) and b == 0 and u < RING):
                    dve.wait_ge(den_ready, UNITS * b + u - RING + 1)
                for n in range(1):
                    c = cap[:, j, half * NQ:(half + 1) * NQ].unsqueeze(1).to_broadcast([P, 2, NQ])
                    dve.scalar_tensor_tensor(out=probs[:, u % RING, 2 * pair:2 * pair + 2, :], in0=ps_s[pair][:, :, :],
                                             scalar=-CLIP, in1=c, op0=ALU.max, op1=ALU.min).then_inc(clipped, 1)

            def scale(b, par, u):
                half, j = divmod(u, NC)
                dve.wait_ge(recip_ready, UNITS * b + u + 1)
                dve.wait_ge(ctx_ready, UNITS * b + u + 1)
                dst = ctxT[par][:, half * NQ:(half + 1) * NQ] if j == 0 else prod[:, u % 2, :]
                if j == 0:
                    if not (isinstance(b, int) and b < 2):
                        pass
                if j >= 3 or (j in (1, 2) and half == 1):
                    n = 7 * half + j - 2 if j >= 3 else 7
                    dve.wait_ge(summed, 14 * b + n)
                elif j in (1, 2) and not (isinstance(b, int) and b == 0):
                    dve.wait_ge(summed, 14 * b)
                dve.tensor_tensor(dst, ps_c[u % 2][:, :], recip[:, u % 2, :], ALU.mult).then_inc(scaled, 1)

            def statistics(src, st, mv, done):
                for t in range(T):
                    ins = dve.bn_stats(st[:, t, :], src[:, t, :])
                plain_step(ins)
                for t in range(T):
                    ins = dve.bn_aggr(mv[:, t, :], st[:, t, :])
                ins.then_inc(done, 1)

            def normalise(dst, src, mv, rs, done):
                for t in range(T):
                    ins = dve.tensor_scalar(dst[:, t, :], src[:, t, :], mv[:, t, 0:1], rs[:, t:t + 1],
                                            ALU.subtract, ALU.mult)
                ins.then_inc(done, 1)

            def stats_of_x(b):
                dve.wait_ge(x_loaded, 16 * (b + 1))
                statistics(x_in, st_x, mv_x, stats_x)

            def norm_of_x(b):
                dve.wait_ge(rstd_x, b + 1)
                if not (isinstance(b, int) and b == 0):
                    dve.wait_ge(xnbo_ready, b)
                normalise(xn, x_in, mv_x, rs_x, xn_ready)

            def take(kind, half, b, par):
                if kind == "v":
                    dve.wait_ge(v_ready, 2 * b + half + 1)
                    dst = v_sb[par][:, 4 * half:4 * half + 4, :]
                    dve.tensor_tensor(dst, ps_x[:, :].rearrange("p (t d) -> p t d", t=4),
                                      b_v[:, :].unsqueeze(1).to_broadcast([P, 4, D]), ALU.add).then_inc(v_taken, 1)
                elif kind == "wo":
                    dve.wait_ge(wo_ready, 2 * b + half + 1)
                    dve.wait_ge(xnbo_ready, b + 1)
                    if not (isinstance(b, int) and b == 0):
                        dve.wait_ge(x2_stored, 16 * b)
                    dve.tensor_tensor(g[:, 4 * half:4 * half + 4, :], ps_x[:, :].rearrange("p (t d) -> p t d", t=4),
                                      xn_bo[par][:, 4 * half:4 * half + 4, :], ALU.add).then_inc(wo_taken, 1)
                elif kind == "gate":
                    dve.wait_ge(gate_ready, b + 1)
                    dve.tensor_tensor(logit[:, :, :], ps_x[:, 0:T * EX].rearrange("p (t e) -> p t e", e=EX),
                                      b_g[:, :].unsqueeze(1).to_broadcast([P, T, EX]), ALU.add).then_inc(gate_taken, 1)

            def gates(b):
                wait_apart(dve, gate_taken, b + 1)
                for t in range(T):
                    ins = dve.max(top[:, t, :], logit[:, t, :])
                plain_step(ins)
                for t in range(T):
                    ins = dve.max_index(topi[:, t, :], top[:, t, :], logit[:, t, :])
                step(ins)
                dve.tensor_tensor(gap[:, :], top[:, :, 1], top[:, :, 0], ALU.subtract).then_inc(gap_ready, 1)
                step(dve.tensor_copy(topf[:, :, :], topi[:, :, 0:2]))
                dve.wait_ge(egap_ready, b + 1)
                step(dve.tensor_scalar(wgt[:, :, 1], egap[:, :], 1.0, None, ALU.add))
                step(dve.reciprocal(wgt[:, :, 0], wgt[:, :, 1]))
                step(dve.tensor_tensor(wgt[:, :, 1], egap[:, :], wgt[:, :, 0], ALU.mult))
                for k in range(2):
                    ins = dve.tensor_tensor(hot[:, k, :, :], iota_e[:, :].unsqueeze(1).to_broadcast([P, T, EX]),
                                            topf[:, :, k:k + 1].to_broadcast([P, T, EX]), ALU.is_equal)
                step(ins)
                for k in range(2):
                    ins = dve.tensor_tensor(hot[:, k, :, :], hot[:, k, :, :],
                                            wgt[:, :, k:k + 1].to_broadcast([P, T, EX]), ALU.mult)
                step(ins)
                dve.tensor_tensor(wd_all[:, bass.ds(b * T, T), :], hot[:, 0, :, :], hot[:, 1, :, :],
                                  ALU.add).then_inc(weights_ready, 1)

            def stats_of_g(b):
                dve.wait_ge(wo_taken, 2 * b + 2)
                statistics(g, st_g, mv_g, stats_g)

            def norm_of_g(b):
                dve.wait_ge(rstd_g, b + 1)
                normalise(g, g, mv_g, rs_g, tn_ready)

            def stats_of_y(b):
                dve.wait_ge(x2_ready, b + 1)
                statistics(g, st_y, mv_y, stats_y)

            def norm_of_y(b):
                dve.wait_ge(rstd_y, b + 1)
                if not (isinstance(b, int) and b == 0):
                    dve.wait_ge(yT_ready, 2 * b)
                normalise(yn, g, mv_y, rs_y, yn_ready)

            def body(b, par, first=False, last=False):
                for s in range(UNITS):
                    clip(b, s, 0)
                    clip(b, s, 1)
                    if s - 1 in PIECES:
                        kind, half = PIECES[s - 1]
                        if piece_runs(kind, first, last) and kind in ("v", "wo", "gate"):
                            take(kind, half, b + 1 if kind in NEXT else b - 1, 1 - par)
                    if not (first and s < 3):
                        scale(before(b, s, 3)[0], par if s >= 3 else 1 - par, before(b, s, 3)[1])
                    if not last:
                        if s == 0:
                            stats_of_x(b + 1)
                        if s == 1:
                            norm_of_x(b + 1)
                    if not first:
                        if s == 6:
                            stats_of_g(b - 1)
                        if s == 7:
                            norm_of_g(b - 1)
                        if s == 10:
                            stats_of_y(b - 1)
                        if s == 11:
                            norm_of_y(b - 1)
                        if s == 15:
                            gates(b - 1)

            dve.wait_ge(const_in, 14 * 16)
            dve.tensor_scalar(b_q[:, :], b_q[:, :], SCALE, None, ALU.mult).then_inc(bias_ready, 1)
            dve.memset(ones[:, :], 1.0).then_inc(ones_ready, 1)
            stats_of_x(0)
            norm_of_x(0)
            for j in range(NC):
                dve.wait_ge(adj_in[j % 2], 16 * (j // 2 + 1))
                if j >= 2:
                    dve.wait_ge(cap_ready, j - 1)
                dve.tensor_scalar(hot_buf[j % 2], adj_buf[j % 2], 0.0, None, ALU.not_equal).then_inc(adj_hot, 1)
                if j == 1:
                    take("v", 0, 0, 0)
                    take("v", 1, 0, 0)
            body(0, 0, first=True)
            base = chained[1]
            with dve.Fori(0, (B - 2) // 2) as i:
                chained[0], chained[1] = base + i * DVE_STEPS, 0
                body(2 * i + 1, 1)
                body(2 * i + 2, 0)
                assert chained[1] == DVE_STEPS, chained[1]
            chained[0], chained[1] = base + (B - 2) // 2 * DVE_STEPS, 0
            body(B - 1, 1, last=True)
            for u in range(UNITS - 3, UNITS):
                scale(B - 1, 1, u)
            take("wo", 0, B - 1, 1)
            take("wo", 1, B - 1, 1)
            stats_of_g(B - 1)
            norm_of_g(B - 1)
            stats_of_y(B - 1)
            norm_of_y(B - 1)
            take("gate", 0, B - 1, 1)
            gates(B - 1)

        @block.gpsimd
        def _(pool):
            chained = [0, 0]

            def step(ins):
                chained[1] += 1
                ins.then_inc(pool_step, 1)
                pool.wait_ge(pool_step, chained[0] + chained[1])

            def rstd(rs, mv, stats, done, b):
                wait_apart(pool, stats, b + 1)
                step(pool.tensor_scalar(rs[:, :], mv[:, :, 1], EPS, None, ALU.add))
                pool.tensor_tensor(rs[:, :], rs[:, :], minus_half[:, :], ALU.pow).then_inc(done, 1)

            def add_bo(b, par):
                pool.wait_ge(xn_ready, b + 1)
                pool.tensor_tensor(xn_bo[par][:, :, :], xn[:, :, :], b_o[:, :].unsqueeze(1).to_broadcast([P, T, D]),
                                   ALU.add).then_inc(xnbo_ready, 1)

            def accumulate(b, par, u):
                half, j = divmod(u, NC)
                if j == 0:
                    return
                pool.wait_ge(scaled, UNITS * b + u + 1)
                n = 7 * half + j - 1
                if not (isinstance(b, int) and b == 0 and n == 0):
                    pool.wait_ge(summed, 14 * b + n)
                dst = ctxT[par][:, half * NQ:(half + 1) * NQ]
                pool.tensor_tensor(dst, dst, prod[:, u % 2, :], ALU.add).then_inc(summed, 1)

            def low(b, which, half):
                n = 4 * b + 2 * which + half
                high, lo = (q_part, k_part)[which]
                pool.wait_ge(qk_high, n + 1)
                cols = slice(half * NQ, (half + 1) * NQ)
                pool.tensor_tensor(lo[:, cols], full[:, half, :], high[:, cols].bitcast(F32),
                                   ALU.subtract).then_inc(qk_low, 1)

            def res_beta(b):
                pool.wait_ge(res_loaded, 16 * (b + 1))
                step(pool.tensor_tensor(x_res[:, :, :], x_res[:, :, :], beta[:, :].unsqueeze(1).to_broadcast([P, T, D]),
                                        ALU.add))

            def times_gamma(b):
                pool.wait_ge(tn_ready, b + 1)
                step(pool.tensor_tensor(g[:, :, :], g[:, :, :], gamma[:, :].unsqueeze(1).to_broadcast([P, T, D]),
                                        ALU.mult))

            def residual(b):
                pool.tensor_tensor(g[:, :, :], g[:, :, :], x_res[:, :, :], ALU.add).then_inc(x2_ready, 1)

            def body(b, par, first=False, last=False):
                for s in range(UNITS):
                    if not (first and s < 3):
                        accumulate(before(b, s, 3)[0], par if s >= 3 else 1 - par, before(b, s, 3)[1])
                    if not last:
                        if s == 0:
                            rstd(rs_x, mv_x, stats_x, rstd_x, b + 1)
                        if s == 7:
                            if not first:
                                pool.wait_ge(wo_taken, 2 * b)
                            add_bo(b + 1, 1 - par)
                        if s - 1 in PIECES and PIECES[s - 1][0] in ("q", "k"):
                            kind, half = PIECES[s - 1]
                            low(b + 1, int(kind == "k"), half)
                    if not first:
                        if s == 4:
                            res_beta(b - 1)
                        if s == 6:
                            rstd(rs_g, mv_g, stats_g, rstd_g, b - 1)
                        if s == 7:
                            times_gamma(b - 1)
                        if s == 8:
                            residual(b - 1)
                        if s == 10:
                            rstd(rs_y, mv_y, stats_y, rstd_y, b - 1)

            pool.wait_ge(const_in, 14 * 16)
            step(pool.memset(minus_half[:, :], -0.5))
            rstd(rs_x, mv_x, stats_x, rstd_x, 0)
            add_bo(0, 0)
            for which in range(2):
                for half in range(2):
                    low(0, which, half)
            body(0, 0, first=True)
            base = chained[1]
            with pool.Fori(0, (B - 2) // 2) as i:
                chained[0], chained[1] = base + i * POOL_STEPS, 0
                body(2 * i + 1, 1)
                body(2 * i + 2, 0)
                assert chained[1] == POOL_STEPS, chained[1]
            chained[0], chained[1] = base + (B - 2) // 2 * POOL_STEPS, 0
            body(B - 1, 1, last=True)
            for u in range(UNITS - 3, UNITS):
                accumulate(B - 1, 1, u)
            res_beta(B - 1)
            rstd(rs_g, mv_g, stats_g, rstd_g, B - 1)
            times_gamma(B - 1)
            residual(B - 1)
            rstd(rs_y, mv_y, stats_y, rstd_y, B - 1)


DVE_STEPS = 2 * 11
POOL_STEPS = 2 * 5


def piece_runs(kind, first, last):
    return not last if kind in NEXT else not first


def expert_phase(nc, a, yT_dram, x2_dram, wd_all, out):
    with ExitStack() as ctx:
        def sb(name, shape, dt=F32):
            return ctx.enter_context(nc.sbuf_tensor(name, shape, dt))

        def sem(name):
            return ctx.enter_context(nc.semaphore(name))

        w1 = sb("w1", [P, EX, HID])
        w2 = sb("w2", [P, EX, HB, D])
        b1 = sb("b1", [P, EX * HB])
        b2 = sb("b2", [P, EX, D])
        xt = sb("xt", [P, 2, NQ])
        acc = sb("acc", [P, 2, 4, D])
        hT = sb("hT", [P, 2, HB, NQ])
        y = sb("y", [P, 2, 4, D])
        ps_h = ctx.enter_context(nc.psum_tensor("ps_h", [P, 4, NQ], F32))
        ps_y = ctx.enter_context(nc.psum_tensor("ps_y", [P, 2, NQ], F32))
        w_in = sem("w_in")
        t_in = [sem(f"t_in{i}") for i in range(2)]
        h_ready, h_taken, y_ready, y_taken, biased, mixed = (sem(n) for n in (
            "h_ready", "h_taken", "y_ready", "y_taken", "biased", "mixed"))
        stored = [sem(f"stored{i}") for i in range(2)]
        NB = B * N // NQ
        x2_v = x2_dram.rearrange("(n t p) d -> n p t d", p=P, t=4)
        out_v = out.rearrange("b (m t p) d -> (b m) p t d", p=P, t=4)
        yT_v = yT_dram.rearrange("p (n c) -> n p c", c=NQ)
        block = ctx.enter_context(nc.Block())

        @block.sync
        def _(sp):
            sp.dma_start(w1[:, :, :], a["W1"].rearrange("e p h -> p e h")).then_inc(w_in, 16)
            sp.dma_start(w2[:, :, :, :], a["W2"].rearrange("e (m p) d -> p e m d", p=P)).then_inc(w_in, 16)
            sp.dma_start(b1[:, :], a["b1"]).then_inc(w_in, 16)
            sp.dma_start(b2[:, :, :], a["b2"]).then_inc(w_in, 16)

            def load(n, par):
                sp.dma_start(xt[:, par, :], yT_v[n]).then_inc(t_in[par], 16)
                sp.dma_start(acc[:, par, :, :], x2_v[n]).then_inc(t_in[par], 16)

            load(0, 0)
            load(1, 1)
            with sp.Fori(0, NB // 2 - 1) as i:
                for par in range(2):
                    n = 2 * i + par
                    sp.wait_ge(mixed, EX * n + EX)
                    sp.dma_start(out_v[n], acc[:, par, :, :]).then_inc(stored[par], 16)
                    sp.wait_ge(stored[par], 16 * i + 16)
                    load(n + 2, par)
            for par in range(2):
                n = NB - 2 + par
                sp.wait_ge(mixed, EX * n + EX)
                sp.dma_start(out_v[n], acc[:, par, :, :]).then_inc(stored[par], 16)
            for par in range(2):
                sp.wait_ge(stored[par], 16 * (NB // 2))

        @block.tensor
        def _(pe):
            def up(n, par, e, first):
                for m in range(HB):
                    if not (first and e == 0):
                        pe.wait_ge(h_taken, (EX * n + e) * HB + m - HB + 1)
                    pe.matmul(ps_h[:, m, :], w1[:, e, m * P:(m + 1) * P], xt[:, par, :],
                              start=True, stop=True).then_inc(h_ready, 1)

            def down(n, par, e, first):
                pe.wait_ge(h_taken, (EX * n + e + 1) * HB)
                if not (first and e < 2):
                    pe.wait_ge(y_taken, EX * n + e - 1)
                for t in range(4):
                    for m in range(HB):
                        last = pe.matmul(ps_y[:, e % 2, t * P:(t + 1) * P], hT[:, e % 2, m, t * P:(t + 1) * P],
                                         w2[:, e, m, :], start=(m == 0), stop=(m == HB - 1))
                last.then_inc(y_ready, 1)

            def block_of(n, par, turn, first=False):
                pe.wait_ge(t_in[par], 32 * turn + 32)
                up(n, par, 0, first)
                for e in range(EX):
                    if e + 1 < EX:
                        up(n, par, e + 1, first)
                    down(n, par, e, first)

            pe.wait_ge(w_in, 64)
            block_of(0, 0, 0, first=True)
            block_of(1, 1, 0)
            with pe.Fori(1, NB // 2) as i:
                for par in range(2):
                    block_of(2 * i + par, par, i)

        @block.scalar
        def _(act):
            def gelu(n, e, first):
                for m in range(HB):
                    act.wait_ge(h_ready, (EX * n + e) * HB + m + 1)
                    if m == 0 and not (first and e < 2):
                        act.wait_ge(y_ready, EX * n + e - 1)
                    act.activation(hT[:, e % 2, m, :], ps_h[:, m, :], ACT.Gelu,
                                   bias=b1[:, e * HB + m:e * HB + m + 1]).then_inc(h_taken, 1)

            act.wait_ge(w_in, 64)
            for e in range(EX):
                gelu(0, e, True)
            with act.Fori(1, NB) as i:
                for e in range(EX):
                    gelu(i, e, False)

        @block.vector
        def _(dve):
            def mix(n, par, turn):
                dve.wait_ge(t_in[par], 32 * turn + 32)
                for e in range(EX):
                    dve.wait_ge(y_ready, EX * n + e + 1)
                    dve.tensor_tensor(y[:, e % 2, :, :], ps_y[:, e % 2, :].rearrange("p (t d) -> p t d", t=4),
                                      b2[:, e, :].unsqueeze(1).to_broadcast([P, 4, D]), ALU.add).then_inc(y_taken, 1)
                    dve.wait_ge(y_taken, EX * n + e + 1)
                    if e > 0:
                        dve.wait_ge(mixed, EX * n + e)
                    for t in range(4):
                        last = dve.scalar_tensor_tensor(out=acc[:, par, t, :], in0=y[:, e % 2, t, :],
                                                        scalar=wd_all[:, bass.ds(4 * n + t, 1), e],
                                                        in1=acc[:, par, t, :], op0=ALU.mult, op1=ALU.add)
                    last.then_inc(mixed, 1)

            dve.wait_ge(w_in, 64)
            with dve.Fori(0, NB // 2) as i:
                for par in range(2):
                    mix(2 * i + par, par, i)


def build(nc, a, out):
    yT_dram = nc.dram_tensor("yT_scratch", [P, B * N], F32).ap()
    x2_dram = nc.dram_tensor("x2_scratch", [B * N, D], F32).ap()
    with nc.sbuf_tensor("wd_all", [P, B * T, EX], F32) as wd_all:
        attention_phase(nc, a, yT_dram, x2_dram, wd_all)
        expert_phase(nc, a, yT_dram, x2_dram, wd_all, out)


def kernel(**inputs):
    import numpy as np
    import concourse.bacc as bacc
    from concourse.bass_utils import run_bass_kernel_spmd

    g = {k: np.asarray(v) for k, v in inputs.items()}

    def rows(v):
        return np.ascontiguousarray(np.broadcast_to(v[None], (P,) + v.shape))

    arrays = {
        "x": g["x"], "adjT": np.ascontiguousarray(g["adj"].T),
        "WqT": np.ascontiguousarray(g["L0_gnn_Wq"].T), "WkT": np.ascontiguousarray(g["L0_gnn_Wk"].T),
        "WvT": np.ascontiguousarray(g["L0_gnn_Wv"].T), "WoT": np.ascontiguousarray(g["L0_gnn_Wo"].T),
        "bq": g["L0_gnn_bq"].reshape(P, 1), "bk": g["L0_gnn_bk"].reshape(P, 1),
        "bv": rows(g["L0_gnn_bv"]), "bo": rows(g["L0_gnn_bo"]),
        "gamma": rows(g["L0_gnn_gamma"]), "beta": rows(g["L0_gnn_beta"]),
        "Wg": g["L0_ffn_Wg"], "bg": rows(g["L0_ffn_bg"]),
        "W1": g["L0_ffn_W1"], "W2": g["L0_ffn_W2"],
        "b1": np.ascontiguousarray(g["L0_ffn_b1"].reshape(EX * HB, P).T), "b2": rows(g["L0_ffn_b2"]),
        "ident": np.eye(P, dtype=np.float32), "iota": rows(np.arange(EX, dtype=np.float32)),
    }
    nc = bacc.Bacc("TRN2", target_bir_lowering=False, num_devices=1)
    a = {k: nc.dram_tensor(k + "_dram", v.shape, mybir.dt.from_np(v.dtype), kind="ExternalInput").ap()
         for k, v in arrays.items()}
    out = nc.dram_tensor("out", (B, N, D), F32, kind="ExternalOutput").ap()
    build(nc, a, out)
    r = run_bass_kernel_spmd(nc, [{k + "_dram": v for k, v in arrays.items()}], core_ids=[0])
    return r.results[0]["out"]
```

```python
from contextlib import ExitStack

import concourse.bass as bass
from concourse import mybir

F32 = mybir.dt.float32
F32R = mybir.dt.float32r
BF16 = mybir.dt.bfloat16
I32 = mybir.dt.int32
U32 = mybir.dt.uint32
ALU = mybir.AluOpType
ACT = mybir.ActivationFunctionType

P = 128
B, N, D = 8, 1024, 128
H, DH = 4, 32
NC = N // P
T = N // P
NQ = 512
UNITS = (N // NQ) * NC
NG = UNITS // 4
SLOTS = 2 * UNITS
EX, HID = 8, 512
HB = HID // P
CONSTS = 17
SCALE = float(DH) ** -0.5
CLIP = 10.0
EPS = 1e-5
RING = 4
CRING = 8
GROUP = 4
Q_PARTS = (0, 1, 0, 1)
K_PARTS = (0, 0, 1, 1)
AHEAD, RG = 8, 12
CAP = B * N + P
TP = -(-(B * N // P + EX - 1) // RG) * RG
NT = 2 * TP
PASS_TILES = EX * CAP // P + TP
LIST_TILES = -(-2 * PASS_TILES // P) * P
PIECES = {0: ("cT", 0), 1: ("wo", 0), 2: ("xT", 0), 3: ("xT", 1), 4: ("q", 0), 5: ("q", 1), 6: ("yT", 0),
          7: ("cT", 1), 8: ("wo", 1), 9: ("k", 0), 10: ("k", 1), 11: ("v", 0), 12: ("v", 1), 13: ("yT", 1),
          14: ("gate", 0)}
NEXT = ("xT", "q", "k", "v")


def attention_phase(nc, a, xy_dram, list_dram, fill):
    with ExitStack() as ctx:
        def sb(name, shape, dt=F32):
            return ctx.enter_context(nc.sbuf_tensor(name, shape, dt))

        def pb(name, shape, dt=F32):
            return ctx.enter_context(nc.psum_tensor(name, shape, dt))

        def sem(name):
            return ctx.enter_context(nc.semaphore(name))

        w_q, w_k, w_v, w_o = (sb(n, [P, D]) for n in ("w_q", "w_k", "w_v", "w_o"))
        ident = sb("ident", [P, P])
        w_g = sb("w_g", [P, EX])
        b_q, b_k = sb("b_q", [P, 1]), sb("b_k", [P, 1])
        b_v, b_o, gamma, beta = (sb(n, [P, D]) for n in ("b_v", "b_o", "gamma", "beta"))
        b_g, iota_e = sb("b_g", [P, EX]), sb("iota_e", [P, EX])
        place = sb("place", [P, GROUP, DH])
        minus_half = sb("minus_half", [P, T])
        earlier, every = sb("earlier", [P, P], BF16), sb("every", [P, P], BF16)
        token_no = sb("token_no", [P, B * T], I32)
        cap = sb("cap", [P, NC, N], BF16)
        q_stack = [sb(f"q_stack{i}", [P, H, N], F32R) for i in range(2)]
        k_stack = [sb(f"k_stack{i}", [P, H, N], F32R) for i in range(2)]
        v_sb = [sb(f"v_sb{i}", [P, NC, D]) for i in range(2)]
        ctx_n = [sb(f"ctx_n{i}", [P, T, D]) for i in range(2)]
        xn_bo = [sb(f"xn_bo{i}", [P, T, D]) for i in range(2)]
        x_in, xn, x_res = sb("x_in", [P, T, D]), sb("xn", [P, T, D]), sb("x_res", [P, T, D])
        xnT = sb("xnT", [P, N])
        part = [sb(f"part{i}", [P, N], F32R) for i in range(2)]
        full = sb("full", [P, 2, NQ])
        g, yn, ynT = sb("g", [P, T, D]), sb("yn", [P, T, D]), sb("ynT", [P, N])
        st = sb("st", [P, T, 6])
        mv_x, mv_g, mv_y = (sb(n, [P, T, 2]) for n in ("mv_x", "mv_g", "mv_y"))
        rs_x, rs_g, rs_y = (sb(n, [P, T]) for n in ("rs_x", "rs_g", "rs_y"))
        off_x, off_g, off_y = (sb(n, [P, T]) for n in ("off_x", "off_g", "off_y"))
        logit, top, topi = sb("logit", [P, T, EX]), sb("top", [P, T, 8]), sb("topi", [P, T, 8], U32)
        topf = sb("topf", [P, T, 2])
        gap, egap = sb("gap", [P, T]), sb("egap", [P, T])
        hot = sb("hot", [P, T + 1, 2 * EX], BF16)
        pos, slot_f = sb("pos", [P, T, 2 * EX]), sb("slot_f", [P, T, 2])
        listing = [sb(f"listing{i}", [P, T, 2, 2]) for i in range(2)]
        slot = [sb(f"slot{i}", [P, T, 2], I32) for i in range(2)]
        mark = sb("mark", [P, 2])
        probs = sb("probs", [P, RING, H, NQ])
        ctx_sb = sb("ctx_sb", [P, CRING, NQ])
        den_sb = sb("den_sb", [P, NQ])
        recip = sb("recip", [P, 2, 4, H, GROUP])
        prod = sb("prod", [P, 2, 4, D])
        ctxT = ynT

        ps_s = [pb(f"ps_s{i}", [P, 2, NQ]) for i in range(2)]
        ps_c = pb("ps_c", [P, NQ])
        ps_d = pb("ps_d", [P, NQ])
        ps_t = pb("ps_t", [P, NQ])
        ps_x = pb("ps_x", [P, NQ])

        const_in = sem("const_in")
        adj_in = [sem(f"adj_in{i}") for i in range(2)]
        adj_hot, adj_read = sem("adj_hot"), sem("adj_read")
        cap_ready, place_ready = sem("cap_ready"), sem("place_ready")
        bias_ready = sem("bias_ready")
        x_loaded, res_loaded = sem("x_loaded"), sem("res_loaded")
        stats_x, rstd_x, xn_ready, xnbo_ready = sem("stats_x"), sem("rstd_x"), sem("xn_ready"), sem("xnbo_ready")
        xT_ready, xT_taken = sem("xT_ready"), sem("xT_taken")
        qk_ready, qk_taken, qk_high, qk_low = sem("qk_ready"), sem("qk_taken"), sem("qk_high"), sem("qk_low")
        v_ready, v_taken = sem("v_ready"), sem("v_taken")
        q_copied, stacked = sem("q_copied"), [sem(f"stacked{i}") for i in range(2)]
        scores_ready, clipped, probs_ready = sem("scores_ready"), sem("clipped"), sem("probs_ready")
        ctx_ready, den_ready = sem("ctx_ready"), sem("den_ready")
        ctx_taken, den_taken, denT_ready = sem("ctx_taken"), sem("den_taken"), sem("denT_ready")
        ctxT_ready, recip_ready, scaled, summed = sem("ctxT_ready"), sem("recip_ready"), sem("scaled"), sem("summed")
        cT_ready, cT_taken = sem("cT_ready"), sem("cT_taken")
        wo_ready, wo_taken = sem("wo_ready"), sem("wo_taken")
        stats_g, rstd_g, tn_ready, x2_ready = sem("stats_g"), sem("rstd_g"), sem("tn_ready"), sem("x2_ready")
        stats_y, rstd_y, yn_ready = sem("stats_y"), sem("rstd_y"), sem("yn_ready")
        yT_ready, yT_taken, gate_ready, gate_taken = sem("yT_ready"), sem("yT_taken"), sem("gate_ready"), sem("gate_taken")
        gap_ready, egap_ready, hot_ready = sem("gap_ready"), sem("egap_ready"), sem("hot_ready")
        listing_ready, slots_ready = sem("listing_ready"), sem("slots_ready")
        listed = [sem(f"listed{i}") for i in range(2)]
        listing_free = sem("listing_free")
        x2_stored, yn_stored = sem("x2_stored"), sem("yn_stored")
        pads_in, lists_blank = sem("pads_in"), sem("lists_blank")
        dve_step, pool_step = sem("dve_step"), sem("pool_step")

        x_v = a["x"].rearrange("b (t p) d -> b p t d", p=P)
        xy_v = xy_dram.rearrange("(b t p) d -> b p t d", p=P, t=T)
        adj_v = a["adjT"].rearrange("(j p) n -> j p n", p=P)
        adj_buf = [g[:, :, :].bitcast(I32), yn[:, :, :].bitcast(I32)]
        hot_buf = [x_res[:, :, :], ynT[:, :].rearrange("p (t d) -> p t d", t=T)]

        def wait_apart(eng, s, count):
            if not isinstance(count, int):
                count = eng.snap(count)
                eng.compute_val(count)
            eng.wait_ge(const_in, CONSTS * 16)
            eng.wait_ge(s, count)

        def before(b, s, lag):
            return (b, s - lag) if s >= lag else (b - 1, s - lag + UNITS)

        def lagged(b, s, lag, first, tail):
            return not (first and s < lag) and not (tail and s >= lag)

        def bodies(eng, body, chained=None, steps=0):
            body(0, 0, first=True)
            body(1, 1)
            body(2, 0)
            base = chained[1] if chained else 0
            with eng.Fori(1, (B - 2) // 2) as i:
                pair[0] = i
                if chained:
                    chained[0], chained[1] = i * steps + (base - steps), 0
                body(2 * i + 1, 1)
                body(2 * i + 2, 0)
                assert not chained or chained[1] == steps, chained[1]
            if chained:
                chained[0], chained[1] = base + (B - 4) // 2 * steps, 0
            body(B - 1, 1, last=True)
            body(B, 0, tail=True)

        def has(b, n):
            return not isinstance(b, int) or b >= n

        pair = [None]

        def turn(b, par):
            return b // 2 if isinstance(b, int) else pair[0] + (par == 0)

        block = ctx.enter_context(nc.Block())

        @block.sync
        def _(sp):
            consts = [(ident, "ident"), (w_q, "WqT"), (w_k, "WkT"), (w_v, "WvT"), (w_o, "WoT"), (w_g, "Wg"),
                      (b_q, "bq"), (b_k, "bk"), (b_v, "bv"), (b_o, "bo"), (gamma, "gamma"), (beta, "beta"),
                      (b_g, "bg"), (iota_e, "iota"), (token_no, "token_no"), (fill, "slot0")]

            def load_x(b):
                sp.dma_start(x_in[:, :, :], x_v[b]).then_inc(x_loaded, 16)

            def load_res(b):
                sp.dma_start(x_res[:, :, :], x_v[b]).then_inc(res_loaded, 16)

            def load_adj(j):
                if j >= 2:
                    sp.wait_ge(adj_hot, j - 1)
                sp.dma_start(adj_buf[j % 2], adj_v[j].rearrange("p (t d) -> p t d", t=T)).then_inc(adj_in[j % 2], 16)

            def stack(par, which, b):
                stacks, order = ((q_stack, Q_PARTS), (k_stack, K_PARTS))[which]
                sp.wait_ge(qk_high, 4 * b + 2 * which + 2)
                sp.wait_ge(qk_low, 4 * b + 2 * which + 2)
                for row, p in enumerate(order):
                    for h in range(H):
                        sp.dma_start(stacks[par][DH * row:DH * (row + 1), h, :].bitcast(F32),
                                     part[p][DH * h:DH * (h + 1), :].bitcast(F32))\
                            .then_inc(stacked[par] if which else q_copied, 16)

            load_x(0)
            for dst, name in consts:
                sp.dma_start(dst[:], a[name]).then_inc(const_in, 16)
            sp.dma_start(full[:, 0, 0:P], a["earlier"]).then_inc(const_in, 16)
            load_adj(0)
            load_adj(1)
            sp.wait_ge(xn_ready, 2)
            load_x(1)
            stack(0, 0, 0)
            stack(0, 1, 0)
            for j in range(2, NC):
                load_adj(j)
            sp.dma_start(den_sb[:, 0:2 * P], a["pads"]).then_inc(pads_in, 16)
            sp.wait_ge(pads_in, 16)
            sp.dma_start(list_dram.rearrange("(p n q) c -> p n (q c)", p=P, q=P),
                         den_sb[:, 0:2 * P].unsqueeze(1).to_broadcast([P, LIST_TILES // P, 2 * P]))\
                .then_inc(lists_blank, 16)
            sp.wait_ge(cap_ready, NC)
            load_res(0)

            def store(b):
                sp.wait_ge(yn_ready, 2 * b + 2)
                sp.dma_start(xy_v[b][:, :, D:], g[:, :, :]).then_inc(x2_stored, 16)
                sp.dma_start(xy_v[b][:, :, 0:D], yn[:, :, :]).then_inc(yn_stored, 16)

            def body(b, par, first=False, last=False):
                if not last:
                    if not first:
                        sp.wait_ge(scores_ready, SLOTS * b)
                    stack(1 - par, 0, b + 1)
                    stack(1 - par, 1, b + 1)
                if not first:
                    store(b - 1)
                    load_res(b)

            def whole(b, par, first=False):
                sp.wait_ge(xn_ready, 2 * b + 4)
                load_x(b + 2)
                body(b, par, first)

            whole(0, 0, first=True)
            with sp.Fori(0, (B - 4) // 2) as i:
                whole(2 * i + 1, 1)
                whole(2 * i + 2, 0)
            whole(B - 3, 1)
            body(B - 2, 0)
            body(B - 1, 1, last=True)
            store(B - 1)
            sp.wait_ge(x2_stored, 16 * B)
            sp.wait_ge(yn_stored, 16 * B)

        @block.tensor
        def _(pe):
            def spare_free(b, s, runs):
                before_ = [k for k in sorted(PIECES) if k < s and runs(PIECES[k][0])]
                if before_:
                    taken(*PIECES[before_[-1]], b)
                else:
                    pe.wait_ge(v_taken, 2 * min(b, B - 1) + 2 if isinstance(b, int) else 2 * b + 2)
                    if not (isinstance(b, int) and b == 0):
                        pe.wait_ge(gate_taken, b)

            def taken(kind, half, b):
                sem_, count = {"xT": (xT_taken, 2 * (b + 1)), "wo": (wo_taken, 2 * (b - 1)),
                               "cT": (cT_taken, 2 * (b - 1)),
                               "q": (qk_taken, 4 * (b + 1)), "k": (qk_taken, 4 * (b + 1) + 2),
                               "v": (v_taken, 2 * (b + 1)), "yT": (yT_taken, 2 * (b - 1)),
                               "gate": (gate_taken, b)}[kind]
                pe.wait_ge(sem_, count + half + 1)

            def piece(kind, half, b, par):
                lo = half * NQ
                if kind == "xT":
                    pe.wait_ge(xn_ready, 2 * b + half + 1)
                    for t in range(4):
                        last = pe.transpose(ps_x[:, t * P:(t + 1) * P], xn[:, 4 * half + t, :], ident[:, :])
                    last.then_inc(xT_ready, 1)
                elif kind in "qk":
                    pe.wait_ge(xT_taken, 2 * b + half + 1)
                    w = w_q if kind == "q" else w_k
                    pe.matmul(ps_x[:, :], w[:, :], xnT[:, lo:lo + NQ], start=True, stop=True).then_inc(qk_ready, 1)
                elif kind == "v":
                    for t in range(4):
                        last = pe.matmul(ps_x[:, t * P:(t + 1) * P], xnT[:, lo + t * P:lo + (t + 1) * P], w_v[:, :],
                                         start=True, stop=True)
                    last.then_inc(v_ready, 1)
                elif kind == "cT":
                    pe.wait_ge(summed, 14 * b + 7 * (half + 1))
                    for t in range(4):
                        last = pe.transpose(ps_x[:, t * P:(t + 1) * P], ctx_n[par][:, 4 * half + t, :], ident[:, :])
                    last.then_inc(cT_ready, 1)
                elif kind == "wo":
                    pe.wait_ge(cT_taken, 2 * b + half + 1)
                    for t in range(4):
                        last = pe.matmul(ps_x[:, t * P:(t + 1) * P], ctxT[:, lo + t * P:lo + (t + 1) * P], w_o[:, :],
                                         start=True, stop=True)
                    last.then_inc(wo_ready, 1)
                elif kind == "yT":
                    pe.wait_ge(yn_ready, 2 * b + half + 1)
                    for t in range(4):
                        last = pe.transpose(ps_x[:, t * P:(t + 1) * P], yn[:, 4 * half + t, :], ident[:, :])
                    last.then_inc(yT_ready, 1)
                else:
                    pe.wait_ge(yT_taken, 2 * b + 2)
                    for t in range(T):
                        last = pe.matmul(ps_x[:, t * EX:(t + 1) * EX], ynT[:, t * P:(t + 1) * P], w_g[:, :],
                                         start=True, stop=True)
                    if has(b, 1):
                        last = ranks(b - 1)
                    last.then_inc(gate_ready, 1)

            def ranks(b):
                rank = ps_x[:, T * EX:T * EX + (T + 1) * 2 * EX].rearrange("p (t c) -> p t c", c=2 * EX)
                pe.wait_ge(hot_ready, b + 1)
                pe.matmul(rank, earlier[:, :], hot[:, :, :], start=True, stop=False)
                for t in range(T):
                    last = pe.matmul(rank[:, t + 1:, :], every[:, :],
                                     hot[:, t:t + 1, :].to_broadcast([P, T - t, 2 * EX]), start=False, stop=(t == T - 1))
                return last

            def scores(b, par, u, hp):
                half, j = divmod(u, NC)
                slot = 2 * u + hp
                if not (isinstance(b, int) and b == 0 and slot < 2):
                    pe.wait_ge(clipped, SLOTS * b + slot - 1)
                for n in range(2):
                    h = 2 * hp + n
                    last = pe.matmul(ps_s[hp][:, n, :], k_stack[par][:, h, j * P:(j + 1) * P],
                                     q_stack[par][:, h, half * NQ:(half + 1) * NQ], start=True, stop=True)
                last.then_inc(scores_ready, 1)

            def context(b, par, u):
                j = u % NC
                pe.wait_ge(probs_ready, SLOTS * b + 2 * u + 2)
                if not (isinstance(b, int) and b == 0 and u < 1):
                    pe.wait_ge(ctx_taken, UNITS * b + u)
                for h in range(H):
                    last = pe.matmul(ps_c[DH * h:DH * (h + 1), :], v_sb[par][:, j, DH * h:DH * (h + 1)],
                                     probs[:, u % RING, h, :], start=True, stop=True, tile_position=(0, DH * h))
                last.then_inc(ctx_ready, 1)

            def denominators(b, u):
                g_ = u % GROUP
                if g_ == 0 and not (isinstance(b, int) and b == 0 and u < GROUP):
                    pe.wait_ge(den_taken, NG * b + u // GROUP)
                for h in range(H):
                    last = pe.matmul(ps_d[DH * h:DH * (h + 1), :], place[:, g_, :], probs[:, u % RING, h, :],
                                     start=(g_ == 0), stop=(g_ == GROUP - 1), tile_position=(0, DH * h))
                last.then_inc(den_ready, 1)

            def transpose_den(b, group):
                pe.wait_ge(den_taken, NG * b + group + 1)
                if not (isinstance(b, int) and b == 0 and group == 0):
                    pe.wait_ge(scaled, UNITS * b + GROUP * group)
                for t in range(4):
                    last = pe.transpose(ps_t[:, t * P:(t + 1) * P], den_sb[:, t * P:(t + 1) * P], ident[:, :])
                last.then_inc(denT_ready, 1)

            def transpose_ctx(b, u):
                pe.wait_ge(ctx_taken, UNITS * b + u + 1)
                pe.wait_ge(recip_ready, NG * b + u // GROUP + 1)
                if u % GROUP:
                    pe.wait_ge(scaled, UNITS * b + u)
                for t in range(4):
                    last = pe.transpose(ps_t[:, t * P:(t + 1) * P], ctx_sb[:, u % CRING, t * P:(t + 1) * P], ident[:, :])
                last.then_inc(ctxT_ready, 1)

            def body(b, par, first=False, last=False, tail=False):
                def runs(kind):
                    return not (last or tail) if kind in NEXT else not first

                if not tail:
                    pe.wait_ge(q_copied, 256 * (b + 1))
                    pe.wait_ge(stacked[par], 256 * (turn(b, par) + 1))
                    pe.wait_ge(v_taken, 2 * b + 2)
                for s in range(UNITS):
                    bb, u = before(b, s, 2)
                    if not tail:
                        scores(b, par, s, 0)
                    if lagged(b, s, 2, first, tail):
                        context(bb, par if s >= 2 else 1 - par, u)
                    if not tail:
                        scores(b, par, s, 1)
                    if s % GROUP == 2 and lagged(b, s, 6, first, tail):
                        transpose_den(before(b, s, 6)[0], before(b, s, 6)[1] // GROUP)
                    if lagged(b, s, 2, first, tail):
                        denominators(bb, u)
                    if s in PIECES:
                        kind, half = PIECES[s]
                        if runs(kind):
                            spare_free(b, s, runs)
                            piece(kind, half, b + 1 if kind in NEXT else b - 1, 1 - par)
                    if lagged(b, s, 6, first, tail):
                        transpose_ctx(*before(b, s, 6))

            pe.wait_ge(const_in, CONSTS * 16)
            prev = None
            for kind in ("xT", "q", "k", "v"):
                for half in range(2):
                    if prev is not None:
                        taken(prev[0], prev[1], -1)
                    piece(kind, half, 0, 0)
                    prev = (kind, half)
            pe.wait_ge(place_ready, 1)
            bodies(pe, body)
            pe.wait_ge(gate_taken, B + 1)
            ranks(B - 1).then_inc(gate_ready, 1)

        @block.scalar
        def _(act):
            def probabilities(b, u, pair):
                act.wait_ge(clipped, SLOTS * b + 2 * u + pair + 1)
                buf = probs[:, u % RING, 2 * pair:2 * pair + 2, :]
                act.activation(buf, buf, ACT.Exp).then_inc(probs_ready, 1)

            def take_context(b, u):
                act.wait_ge(ctx_ready, UNITS * b + u + 1)
                if not (isinstance(b, int) and b == 0 and u < CRING):
                    act.wait_ge(ctxT_ready, UNITS * b + u - CRING + 1)
                act.activation(ctx_sb[:, u % CRING, :], ps_c[:, :], ACT.Copy).then_inc(ctx_taken, 1)

            def take_den(b, group):
                act.wait_ge(den_ready, UNITS * b + GROUP * (group + 1))
                if isinstance(b, int) and b == 0 and group == 0:
                    act.wait_ge(lists_blank, 16)
                else:
                    act.wait_ge(denT_ready, NG * b + group)
                act.activation(den_sb[:, :], ps_d[:, :], ACT.Copy).then_inc(den_taken, 1)

            def take(kind, half, b):
                lo = half * NQ
                if kind == "xT":
                    act.wait_ge(xT_ready, 2 * b + half + 1)
                    act.activation(xnT[:, lo:lo + NQ], ps_x[:, :], ACT.Copy).then_inc(xT_taken, 1)
                elif kind in ("q", "k"):
                    n = 4 * b + 2 * (kind == "k") + half
                    act.wait_ge(qk_ready, n + 1)
                    if not (isinstance(b, int) and b == 0 and kind == "q"):
                        act.wait_ge(qk_low, n - 1)
                    act.activation(full[:, half, :], ps_x[:, :], ACT.Identity, bias=(b_q if kind == "q" else b_k)[:, :],
                                   scale=SCALE if kind == "q" else 1.0).then_inc(qk_taken, 1)
                    act.wait_ge(qk_taken, n + 1)
                    for w in copied[0]:
                        act.wait_ge(*w)
                    act.activation(part[0][:, lo:lo + NQ], full[:, half, :], ACT.Copy).then_inc(qk_high, 1)
                elif kind == "cT":
                    act.wait_ge(cT_ready, 2 * b + half + 1)
                    if not (isinstance(b, int) and b == 0):
                        act.wait_ge(gate_ready, b)
                    act.activation(ctxT[:, lo:lo + NQ], ps_x[:, :], ACT.Copy).then_inc(cT_taken, 1)
                elif kind == "yT":
                    act.wait_ge(yT_ready, 2 * b + half + 1)
                    act.activation(ynT[:, lo:lo + NQ], ps_x[:, :], ACT.Copy).then_inc(yT_taken, 1)

            copied = [()]

            def normalise(dst, src, rs, off, done):
                for t in range(src.shape[1]):
                    ins = act.activation(dst[:, t, :], src[:, t, :], ACT.Identity, bias=off[:, t:t + 1],
                                         scale=rs[:, t:t + 1])
                ins.then_inc(done, 1)

            def norm_of_x(b, half):
                act.wait_ge(rstd_x, b + 1)
                if not (isinstance(b, int) and b == 0):
                    act.wait_ge(xnbo_ready, b)
                t = slice(4 * half, 4 * half + 4)
                normalise(xn[:, t, :], x_in[:, t, :], rs_x[:, t], off_x[:, t], xn_ready)

            def norm_of_g(b, half):
                act.wait_ge(rstd_g, 2 * b + half + 1)
                t = slice(4 * half, 4 * half + 4)
                normalise(g[:, t, :], g[:, t, :], rs_g[:, t], off_g[:, t], tn_ready)

            def norm_of_y(b, half):
                act.wait_ge(rstd_y, 2 * b + half + 1)
                if not (isinstance(b, int) and b == 0):
                    act.wait_ge(yT_ready, 2 * b)
                    act.wait_ge(yn_stored, 16 * b)
                t = slice(4 * half, 4 * half + 4)
                normalise(yn[:, t, :], g[:, t, :], rs_y[:, t], off_y[:, t], yn_ready)

            def gap_exp(b):
                act.wait_ge(gap_ready, b + 1)
                act.activation(egap[:, :], gap[:, :], ACT.Exp).then_inc(egap_ready, 1)

            def body(b, par, first=False, last=False, tail=False):
                def runs(kind):
                    return not (last or tail) if kind in NEXT else not first

                for s in range(UNITS):
                    if s - 1 in PIECES:
                        kind, half = PIECES[s - 1]
                        if runs(kind):
                            copied[0] = ((stacked[par], 256 * (turn(b, par) + 1)),)
                            if kind == "k":
                                copied[0] = ((q_copied, 256 * (b + 2)),)
                            take(kind, half, b + 1 if kind in NEXT else b - 1)
                    if s % GROUP == 2 and lagged(b, s, 6, first, tail):
                        take_den(before(b, s, 6)[0], before(b, s, 6)[1] // GROUP)
                    if not tail:
                        probabilities(b, s, 0)
                    if lagged(b, s, 2, first, tail):
                        take_context(*before(b, s, 2))
                    if not tail:
                        probabilities(b, s, 1)
                    if runs("xT") and s in (1, 2):
                        norm_of_x(b + 1, s - 1)
                    if not first:
                        for half, at in enumerate((2, 9)):
                            if s == at + 1:
                                norm_of_g(b - 1, half)
                            if s == at + 3:
                                norm_of_y(b - 1, half)
                    if s == 3 and has(b, 2):
                        gap_exp(b - 2)

            act.wait_ge(bias_ready, 1)
            for half in range(2):
                norm_of_x(0, half)
            for kind in ("xT", "q", "k"):
                copied[0] = ((q_copied, 256),) if kind == "k" else ()
                for half in range(2):
                    take(kind, half, 0)
            for j in range(NC):
                act.wait_ge(adj_hot, j + 1)
                act.activation(cap[:, j, :].rearrange("p (t d) -> p t d", t=T), hot_buf[j % 2], ACT.Copy,
                               bias=-CLIP, scale=2 * CLIP).then_inc(cap_ready, 1)
            bodies(act, body)
            gap_exp(B - 1)

        @block.vector
        def _(dve):
            chained = [0, 0]

            def step(ins):
                chained[1] += 1
                ins.then_inc(dve_step, 1)
                dve.wait_ge(dve_step, chained[0] + chained[1])

            def plain_step(ins):
                chained[1] += 1
                ins.then_inc(dve_step, 1)
                wait_apart(dve, dve_step, chained[0] + chained[1])

            def clip(b, u, hp):
                half, j = divmod(u, NC)
                dve.wait_ge(scores_ready, SLOTS * b + 2 * u + hp + 1)
                if isinstance(b, int) and b == 0 and half == 0:
                    dve.wait_ge(cap_ready, j + 1)
                if not (isinstance(b, int) and b == 0 and u < RING):
                    dve.wait_ge(den_ready, UNITS * b + u - RING + 1)
                c = cap[:, j, half * NQ:(half + 1) * NQ].unsqueeze(1).to_broadcast([P, 2, NQ])
                dve.scalar_tensor_tensor(out=probs[:, u % RING, 2 * hp:2 * hp + 2, :], in0=ps_s[hp][:, :, :],
                                         scalar=-CLIP, in1=c, op0=ALU.max, op1=ALU.min).then_inc(clipped, 1)

            def invert(b, group):
                dve.wait_ge(denT_ready, NG * b + group + 1)
                den = ps_t[:, :].rearrange("p (t h g r) -> p t h g r", t=4, h=H, g=GROUP)[:, :, :, :, 0]
                dve.reciprocal(recip[:, group % 2, :, :, :], den).then_inc(recip_ready, 1)

            def scale(b, par, u):
                half, j = divmod(u, NC)
                group, g_ = divmod(u, GROUP)
                dve.wait_ge(recip_ready, NG * b + group + 1)
                dve.wait_ge(ctxT_ready, UNITS * b + u + 1)
                dst = ctx_n[par][:, 4 * half:4 * half + 4, :] if j == 0 else prod[:, u % 2, :, :]
                if j >= 3 or (j in (1, 2) and half == 1):
                    n = 7 * half + j - 2 if j >= 3 else 7
                    dve.wait_ge(summed, 14 * b + n)
                elif j in (1, 2) and not (isinstance(b, int) and b == 0):
                    dve.wait_ge(summed, 14 * b)
                r = recip[:, group % 2, :, :, g_].rearrange("p t h -> p (t h)").unsqueeze(2).to_broadcast([P, 4 * H, DH])
                dve.tensor_tensor(dst.rearrange("p t (h d) -> p (t h) d", d=DH), ps_t[:, :].rearrange("p (t d) -> p t d", d=DH),
                                  r, ALU.mult).then_inc(scaled, 1)

            def statistics(src, st, mv, done):
                for t in range(src.shape[1]):
                    ins = dve.bn_stats(st[:, t, :], src[:, t, :])
                plain_step(ins)
                for t in range(src.shape[1]):
                    ins = dve.bn_aggr(mv[:, t, :], st[:, t, :])
                ins.then_inc(done, 1)

            def stats_of_x(b):
                dve.wait_ge(x_loaded, 16 * (b + 1))
                statistics(x_in, st, mv_x, stats_x)

            def take(kind, half, b, par):
                if kind == "v":
                    dve.wait_ge(v_ready, 2 * b + half + 1)
                    dst = v_sb[par][:, 4 * half:4 * half + 4, :]
                    dve.tensor_tensor(dst, ps_x[:, :].rearrange("p (t d) -> p t d", t=4),
                                      b_v[:, :].unsqueeze(1).to_broadcast([P, 4, D]), ALU.add).then_inc(v_taken, 1)
                elif kind == "wo":
                    dve.wait_ge(wo_ready, 2 * b + half + 1)
                    dve.wait_ge(xnbo_ready, b + 1)
                    if not (isinstance(b, int) and b == 0):
                        dve.wait_ge(x2_stored, 16 * b)
                    dve.tensor_tensor(g[:, 4 * half:4 * half + 4, :], ps_x[:, :].rearrange("p (t d) -> p t d", t=4),
                                      xn_bo[par][:, 4 * half:4 * half + 4, :], ALU.add).then_inc(wo_taken, 1)
                elif kind == "gate":
                    dve.wait_ge(gate_ready, b + 1)
                    if has(b, 1):
                        take_ranks(b - 1)
                    dve.tensor_tensor(logit[:, :, :], ps_x[:, 0:T * EX].rearrange("p (t e) -> p t e", e=EX),
                                      b_g[:, :].unsqueeze(1).to_broadcast([P, T, EX]), ALU.add).then_inc(gate_taken, 1)

            def choose(b):
                wait_apart(dve, gate_taken, b + 2)
                for t in range(T):
                    ins = dve.max(top[:, t, :], logit[:, t, :])
                plain_step(ins)
                for t in range(T):
                    ins = dve.max_index(topi[:, t, :], top[:, t, :], logit[:, t, :])
                step(ins)
                dve.tensor_tensor(gap[:, :], top[:, :, 1], top[:, :, 0], ALU.subtract).then_inc(gap_ready, 1)
                step(dve.tensor_copy(topf[:, :, :], topi[:, :, 0:2]))
                if has(b, 1):
                    dve.wait_ge(slots_ready, b)
                for k in range(2):
                    ins = dve.tensor_tensor(hot[:, 0:T, k * EX:(k + 1) * EX],
                                            iota_e[:, :].unsqueeze(1).to_broadcast([P, T, EX]),
                                            topf[:, :, k:k + 1].to_broadcast([P, T, EX]), ALU.is_equal)
                ins.then_inc(hot_ready, 1)

            def entries(b, par):
                entry = listing[par]
                dve.wait_ge(egap_ready, b + 1)
                dve.wait_ge(listing_free, b + 1)
                step(dve.tensor_scalar(entry[:, :, 1, 1], egap[:, :], 1.0, None, ALU.add))
                step(dve.reciprocal(entry[:, :, 0, 1], entry[:, :, 1, 1]))
                dve.tensor_tensor(entry[:, :, 1, 1], egap[:, :], entry[:, :, 0, 1], ALU.mult)
                dve.tensor_copy(entry[:, :, :, 0].bitcast(I32),
                                token_no[:, bass.ds(b * T, T)].unsqueeze(2).to_broadcast([P, T, 2]))\
                    .then_inc(listing_ready, 1)

            def take_ranks(b):
                dve.wait_ge(gate_ready, b + 2)
                rank = ps_x[:, T * EX:T * EX + (T + 1) * 2 * EX].rearrange("p (t c) -> p t c", c=2 * EX)
                flat_fill = fill[:, :, :].rearrange("p k e -> p (k e)")
                step(dve.tensor_tensor(pos[:, :, :], rank[:, 0:T, :],
                                       flat_fill.unsqueeze(1).to_broadcast([P, T, 2 * EX]), ALU.add))
                step(dve.tensor_tensor(flat_fill, flat_fill, rank[:, T, :], ALU.add))

            def slots(b, par):
                step(dve.tensor_tensor(pos[:, :, :], pos[:, :, :], hot[:, 0:T, :], ALU.mult))
                step(dve.tensor_reduce(slot_f[:, :, :], pos[:, :, :].rearrange("p t (k e) -> p t k e", k=2),
                                       mybir.AxisListType.X, ALU.add))
                dve.tensor_copy(slot[par][:, :, :], slot_f[:, :, :]).then_inc(slots_ready, 1)

            def halves(half):
                return slice(4 * half, 4 * half + 4)

            def stats_of_g(b, half):
                dve.wait_ge(wo_taken, 2 * b + half + 1)
                statistics(g[:, halves(half), :], st[:, halves(half), :], mv_g[:, halves(half), :], stats_g)

            def stats_of_y(b, half):
                dve.wait_ge(x2_ready, 2 * b + half + 1)
                statistics(g[:, halves(half), :], st[:, halves(half), :], mv_y[:, halves(half), :], stats_y)

            def body(b, par, first=False, last=False, tail=False):
                def runs(kind):
                    return not (last or tail) if kind in NEXT else not first

                for s in range(UNITS):
                    if not tail:
                        clip(b, s, 0)
                    if lagged(b, s, 7, first, tail):
                        scale(before(b, s, 7)[0], par if s >= 7 else 1 - par, before(b, s, 7)[1])
                    if s - 1 in PIECES:
                        kind, half = PIECES[s - 1]
                        if runs(kind) and kind in ("v", "wo", "gate"):
                            take(kind, half, b + 1 if kind in NEXT else b - 1, 1 - par)
                    if not tail:
                        clip(b, s, 1)
                    if s % GROUP == 2 and lagged(b, s, 6, first, tail):
                        invert(before(b, s, 6)[0], before(b, s, 6)[1] // GROUP)
                    if runs("xT") and s == 0:
                        stats_of_x(b + 1)
                    if not first:
                        for half, at in enumerate((2, 9)):
                            if s == at:
                                stats_of_g(b - 1, half)
                            if s == at + 2:
                                stats_of_y(b - 1, half)
                    if has(b, 2):
                        if s == 1:
                            choose(b - 2)
                        if s == 7:
                            entries(b - 2, par)
                        if s == UNITS - 1:
                            slots(b - 2, par)

            dve.wait_ge(const_in, CONSTS * 16)
            dve.tensor_copy(earlier[:, :], full[:, 0, 0:P])
            dve.tensor_scalar(b_q[:, :], b_q[:, :], SCALE, None, ALU.mult).then_inc(bias_ready, 1)
            dve.memset(every[:, :], 1.0)
            dve.memset(hot[:, T, :], 0.0)
            step(dve.memset(place[:, :, :], 0.0))
            for g_ in range(GROUP):
                ins = dve.memset(place[:, g_, DH // GROUP * g_:DH // GROUP * (g_ + 1)], 1.0)
            ins.then_inc(place_ready, 1)
            dve.memset(gap[:, :], 0.0).then_inc(gate_taken, 1)
            stats_of_x(0)
            for j in range(NC):
                dve.wait_ge(adj_in[j % 2], 16 * (j // 2 + 1))
                if j >= 2:
                    dve.wait_ge(cap_ready, j - 1)
                dve.tensor_scalar(hot_buf[j % 2], adj_buf[j % 2], 0.0, None, ALU.not_equal).then_inc(adj_hot, 1)
                if j == 1:
                    take("v", 0, 0, 0)
                    take("v", 1, 0, 0)
            bodies(dve, body, chained, DVE_STEPS)
            choose(B - 1)
            entries(B - 1, 1)
            take_ranks(B - 1)
            slots(B - 1, 1)

        @block.gpsimd
        def _(pool):
            chained = [0, 0]

            def step(ins):
                chained[1] += 1
                ins.then_inc(pool_step, 1)
                pool.wait_ge(pool_step, chained[0] + chained[1])

            def rstd(rs, off, mv, stats, done, count):
                wait_apart(pool, stats, count)
                pool.tensor_scalar(off, mv[:, :, 0], -1.0, None, ALU.mult)
                step(pool.tensor_scalar(rs, mv[:, :, 1], EPS, None, ALU.add))
                step(pool.tensor_tensor(rs, rs, minus_half[:, 0:rs.shape[1]], ALU.pow))
                pool.tensor_tensor(off, off, rs, ALU.mult).then_inc(done, 1)

            def add_bo(b, par):
                pool.wait_ge(xn_ready, 2 * b + 2)
                pool.tensor_tensor(xn_bo[par][:, :, :], xn[:, :, :], b_o[:, :].unsqueeze(1).to_broadcast([P, T, D]),
                                   ALU.add).then_inc(xnbo_ready, 1)

            def accumulate(b, par, u):
                half, j = divmod(u, NC)
                if j == 0:
                    return
                pool.wait_ge(scaled, UNITS * b + u + 1)
                n = 7 * half + j - 1
                if not (isinstance(b, int) and b == 0 and n == 0):
                    pool.wait_ge(summed, 14 * b + n)
                dst = ctx_n[par][:, 4 * half:4 * half + 4, :]
                pool.tensor_tensor(dst, dst, prod[:, u % 2, :, :], ALU.add).then_inc(summed, 1)

            def low(b, which, half):
                n = 4 * b + 2 * which + half
                high, lo = part
                pool.wait_ge(qk_high, n + 1)
                cols = slice(half * NQ, (half + 1) * NQ)
                pool.tensor_tensor(lo[:, cols], full[:, half, :], high[:, cols].bitcast(F32),
                                   ALU.subtract).then_inc(qk_low, 1)

            def res_beta(b):
                pool.wait_ge(res_loaded, 16 * (b + 1))
                step(pool.tensor_tensor(x_res[:, :, :], x_res[:, :, :], beta[:, :].unsqueeze(1).to_broadcast([P, T, D]),
                                        ALU.add))

            def second_norm(b, half):
                t = slice(4 * half, 4 * half + 4)
                pool.wait_ge(tn_ready, 2 * b + half + 1)
                step(pool.tensor_tensor(g[:, t, :], g[:, t, :], gamma[:, :].unsqueeze(1).to_broadcast([P, 4, D]),
                                        ALU.mult))
                pool.tensor_tensor(g[:, t, :], g[:, t, :], x_res[:, t, :], ALU.add).then_inc(x2_ready, 1)

            def list_entries(b, par, n):
                t, k = divmod(n, 2)
                if n == 0:
                    wait_apart(pool, listing_ready, b + 1)
                    wait_apart(pool, slots_ready, b + 1)
                pool.indirect_dma_start(out=list_dram[:, :],
                                        out_offset=bass.IndirectOffsetOnAxis(ap=slot[par][:, t, k:k + 1], axis=0),
                                        in_=listing[par][:, t, k, :], in_offset=None,
                                        bounds_check=LIST_TILES * P - 1, oob_is_err=False).then_inc(listed[par], 16)

            def all_listed(b, par, times):
                if isinstance(b, int):
                    pool.wait_ge(listing_free, b + 2)
                    pool.wait_ge(listed[par], 256 * times)
                else:
                    wait_apart(pool, listed[par], 256 * times)
                pool.memset(mark[:, par:par + 1], 0.0).then_inc(listing_free, 1)

            def body(b, par, first=False, last=False, tail=False):
                for s in range(UNITS):
                    if has(b, 3):
                        if s < T:
                            list_entries(b - 3, 1 - par, 2 * s)
                            list_entries(b - 3, 1 - par, 2 * s + 1)
                        if s == T + 2:
                            all_listed(b - 3, 1 - par, (b - 3) // 2 + 1 if isinstance(b, int) else pair[0])
                    if not last and not tail:
                        if s == 1:
                            rstd(rs_x[:, :], off_x[:, :], mv_x, stats_x, rstd_x, b + 2)
                        if s == 10:
                            if not first:
                                pool.wait_ge(wo_taken, 2 * b)
                            add_bo(b + 1, 1 - par)
                        if s - 1 in PIECES and PIECES[s - 1][0] in ("q", "k"):
                            kind, half = PIECES[s - 1]
                            low(b + 1, int(kind == "k"), half)
                    if not first:
                        for half, at in enumerate((2, 9)):
                            t = slice(4 * half, 4 * half + 4)
                            if s == at + 1:
                                rstd(rs_g[:, t], off_g[:, t], mv_g[:, t, :], stats_g, rstd_g, 2 * (b - 1) + half + 1)
                            if s == at + 2:
                                second_norm(b - 1, half)
                            if s == at + 3:
                                rstd(rs_y[:, t], off_y[:, t], mv_y[:, t, :], stats_y, rstd_y, 2 * (b - 1) + half + 1)
                        if s == 1:
                            res_beta(b - 1)
                    if lagged(b, s, 7, first, tail):
                        accumulate(before(b, s, 7)[0], par if s >= 7 else 1 - par, before(b, s, 7)[1])

            pool.wait_ge(const_in, CONSTS * 16)
            for par in range(2):
                pool.memset(mark[:, par:par + 1], 0.0).then_inc(listing_free, 1)
            step(pool.memset(minus_half[:, :], -0.5))
            rstd(rs_x[:, :], off_x[:, :], mv_x, stats_x, rstd_x, 1)
            add_bo(0, 0)
            for which in range(2):
                for half in range(2):
                    low(0, which, half)
            pool.wait_ge(lists_blank, 16)
            bodies(pool, body, chained, POOL_STEPS)
            for n in range(2 * T):
                list_entries(B - 2, 0, n)
            for n in range(2 * T):
                list_entries(B - 1, 1, n)
            for par in range(2):
                pool.wait_ge(listed[par], 256 * (B // 2))


DVE_STEPS = 2 * 14
POOL_STEPS = 2 * 13


def expert_phase(nc, a, xy_dram, list_dram, fill, out):
    with ExitStack() as ctx:
        def sb(name, shape, dt=F32):
            return ctx.enter_context(nc.sbuf_tensor(name, shape, dt))

        def pb(name):
            return ctx.enter_context(nc.psum_tensor(name, [P, HID], F32))

        def sem(name):
            return ctx.enter_context(nc.semaphore(name))

        w1, w2 = sb("w1", [P, EX, HID]), sb("w2", [P, EX, HB, D])
        b1, b2 = sb("b1", [P, EX, HID]), sb("b2", [P, EX, D])
        ident = sb("ident_e", [P, P])
        slot0, lower, tile_no, tile_base = (sb("slot0_e", [P, 2, EX]), sb("lower", [P, EX, EX]),
                                            sb("tile_no", [P, TP]), sb("tile_base", [P, 2, TP]))
        tiles = sb("tiles", [P, 2, EX])
        part_sum = sb("part_sum", [P, 2, EX, EX])
        ends = sb("ends", [P, 2, EX])
        gone, gone_tiles = sb("gone", [P, 2, TP, EX]), sb("gone_tiles", [P, 2, TP, EX])
        expert, start = sb("expert", [P, 2, TP]), sb("start", [P, 2, TP])
        expert_of, list_tile = sb("expert_of", [P, NT], I32), sb("list_tile", [P, NT], I32)
        entry = sb("entry", [P, RG, 2])
        rows = sb("rows", [P, RG, 2, D])
        xT = sb("xT", [P, 2, P])
        hid = sb("hid", [P, 2, HID])
        hidT = sb("hidT", [P, 2, HB, P])
        y = sb("y", [P, D])
        ps_x, ps_h, ps_t, ps_y = ([pb(f"{n}{i}") for i in range(2)] for n in ("ps_xT", "ps_h", "ps_hT", "ps_y"))

        w_in, const_in, table_step, table_ready = sem("w_in"), sem("tconst_in"), sem("table_step"), sem("table_ready")
        cleared = sem("cleared")
        entry_in = [sem(f"entry_in{r}") for r in range(RG)]
        gathered = [sem(f"gathered{r}") for r in range(RG)]
        scattered = [sem(f"scattered{r}") for r in range(RG)]
        xT_ready, xT_taken, h_ready, biased = sem("xT_ready_e"), sem("xT_taken_e"), sem("h_ready"), sem("biased")
        gelu_done, hT_ready, hT_taken = sem("gelu_done"), sem("hT_ready"), sem("hT_taken")
        y_ready, y_taken, mixed = sem("y_ready"), sem("y_taken"), sem("mixed")
        block = ctx.enter_context(nc.Block())

        entries = list_dram.rearrange("(n p) c -> n p c", p=P)
        TURNS, PASS_TURNS = NT // RG, TP // RG

        @block.sync
        def _(sp):
            for dst, name in ((slot0, "slot0"), (lower, "lower"), (tile_no, "tile_no"), (tile_base, "tile_base"),
                              (ident, "ident")):
                sp.dma_start(dst[:], a[name]).then_inc(const_in, 16)
            sp.dma_start(w1[:, :, :], a["W1"].rearrange("e p h -> p e h")).then_inc(w_in, 16)
            sp.dma_start(b1[:, :, :], a["b1"]).then_inc(w_in, 16)
            sp.dma_start(w2[:, :, :, :], a["W2"].rearrange("e (m p) d -> p e m d", p=P)).then_inc(w_in, 16)
            sp.dma_start(b2[:, :, :], a["b2"]).then_inc(w_in, 16)

            def load(turn, r, first):
                at = sp.value_load(list_tile[0:1, bass.ds(RG * turn + r, 1)], min_val=0, max_val=LIST_TILES - 1)
                if not first:
                    count = sp.snap(16 * turn)
                    sp.compute_val(count)
                    sp.wait_ge(table_ready, 1)
                    sp.wait_ge(scattered[r], count)
                sp.dma_start(entry[:, r, :], entries[bass.ds(at, 1), :, :].rearrange("o p c -> (o p) c"))\
                    .then_inc(entry_in[r], 16)

            sp.wait_ge(table_ready, 1)
            for r in range(RG):
                load(0, r, True)
            with sp.Fori(1, TURNS) as i:
                for r in range(RG):
                    load(i, r, False)

        @block.gpsimd
        def _(pool):
            token = [entry[:, r, 0:1].bitcast(I32) for r in range(RG)]

            def wait_apart(s, count):
                if not isinstance(count, int):
                    count = pool.snap(count)
                    pool.compute_val(count)
                pool.wait_ge(cleared, 1)
                pool.wait_ge(s, count)

            def gather(k, turn, r):
                wait_apart(entry_in[r], 16 * turn + 16)
                pool.indirect_dma_start(out=rows[:, r, :, :].rearrange("p c d -> p (c d)"), out_offset=None,
                                        in_=xy_dram[k][:, :], in_offset=bass.IndirectOffsetOnAxis(ap=token[r], axis=0),
                                        bounds_check=B * N - 1, oob_is_err=False).then_inc(gathered[r], 16)

            def scatter(k, turn, r):
                wait_apart(mixed, RG * turn + r + 1)
                if k == 0:
                    src, dst = rows[:, r, :, :].rearrange("p c d -> p (c d)"), xy_dram[1][:, :]
                else:
                    src, dst = rows[:, r, 1, :], out.rearrange("b n d -> (b n) d")
                pool.indirect_dma_start(out=dst, out_offset=bass.IndirectOffsetOnAxis(ap=token[r], axis=0),
                                        in_=src, in_offset=None,
                                        bounds_check=B * N - 1, oob_is_err=False).then_inc(scattered[r], 16)

            pool.wait_ge(cleared, 1)
            for k in range(2):
                t0 = k * PASS_TURNS
                if k:
                    for r in range(RG):
                        pool.wait_ge(scattered[r], 16 * t0)
                for r in range(AHEAD):
                    gather(k, t0, r)
                with pool.Fori(t0, t0 + PASS_TURNS - 1) as i:
                    for r in range(RG):
                        gather(k, i + (r + AHEAD) // RG, (r + AHEAD) % RG)
                        scatter(k, i, r)
                for r in range(RG):
                    if r + AHEAD < RG:
                        gather(k, t0 + PASS_TURNS - 1, r + AHEAD)
                    scatter(k, t0 + PASS_TURNS - 1, r)
            for r in range(RG):
                pool.wait_ge(scattered[r], 16 * TURNS)

        @block.tensor
        def _(pe):
            def expert_at(n):
                return pe.value_load(expert_of[0:1, bass.ds(n, 1)], min_val=0, max_val=EX - 1)

            def turn_x(turn, r, n):
                pe.wait_ge(gathered[r], 16 * turn + 16)
                if not isinstance(n, int) or n >= 2:
                    pe.wait_ge(xT_taken, n - 1)
                pe.transpose(ps_x[r % 2][:, 0:P], rows[:, r, 0, :], ident[:, :]).then_inc(xT_ready, 1)

            def up(r, n):
                e = expert_at(n)
                pe.wait_ge(xT_taken, n + 1)
                if not isinstance(n, int) or n >= 2:
                    pe.wait_ge(biased, n - 1)
                pe.matmul(ps_h[r % 2][:, :], xT[:, r % 2, :], w1[:, bass.ds(e, 1), :],
                          start=True, stop=True).then_inc(h_ready, 1)

            def turn_h(r, n):
                pe.wait_ge(gelu_done, n + 1)
                if not isinstance(n, int) or n >= 2:
                    pe.wait_ge(hT_taken, n - 1)
                for m in range(HB):
                    last = pe.transpose(ps_t[r % 2][:, m * P:(m + 1) * P], hid[:, r % 2, m * P:(m + 1) * P], ident[:, :])
                last.then_inc(hT_ready, 1)

            def down(r, n):
                e = expert_at(n)
                pe.wait_ge(hT_taken, n + 1)
                if not isinstance(n, int) or n >= 2:
                    pe.wait_ge(y_taken, n - 1)
                for m in range(HB):
                    last = pe.matmul(ps_y[r % 2][:, 0:D], hidT[:, r % 2, m, :], w2[:, bass.ds(e, 1), m, :],
                                     start=(m == 0), stop=(m == HB - 1))
                last.then_inc(y_ready, 1)

            def turn_of(turn, first=False, last=False):
                for r in range(RG):
                    n = RG * turn + r
                    if not (last and r + 2 >= RG):
                        turn_x(turn + (r + 2) // RG, (r + 2) % RG, n + 2)
                    if not (last and r + 1 >= RG):
                        up((r + 1) % RG, n + 1)
                    turn_h(r, n)
                    if not (first and r == 0):
                        down((r - 1) % RG, n - 1)

            pe.wait_ge(table_ready, 1)
            pe.wait_ge(const_in, 5 * 16)
            pe.wait_ge(w_in, 4 * 16)
            for t0 in (0, PASS_TURNS):
                turn_x(t0, 0, RG * t0)
                turn_x(t0, 1, RG * t0 + 1)
                up(0, RG * t0)
                turn_of(t0, first=True)
                with pe.Fori(t0 + 1, t0 + PASS_TURNS - 1) as i:
                    turn_of(i)
                turn_of(t0 + PASS_TURNS - 1, last=True)
                down(RG - 1, RG * (t0 + PASS_TURNS) - 1)

        @block.scalar
        def _(act):
            def take_x(r, n):
                act.wait_ge(xT_ready, n + 1)
                if not isinstance(n, int) or n >= 2:
                    act.wait_ge(h_ready, n - 1)
                act.activation(xT[:, r % 2, :], ps_x[r % 2][:, 0:P], ACT.Copy).then_inc(xT_taken, 1)

            def gelu(r, n):
                act.wait_ge(biased, n + 1)
                act.activation(hid[:, r % 2, :], hid[:, r % 2, :], ACT.Gelu).then_inc(gelu_done, 1)

            def take_h(r, n):
                act.wait_ge(hT_ready, n + 1)
                if not isinstance(n, int) or n >= 2:
                    act.wait_ge(y_ready, n - 1)
                act.activation(hidT[:, r % 2, :, :], ps_t[r % 2][:, :].rearrange("p (m t) -> p m t", m=HB),
                               ACT.Copy).then_inc(hT_taken, 1)

            def turn_of(turn, last=False):
                for r in range(RG):
                    n = RG * turn + r
                    gelu(r, n)
                    if not (last and r + 2 >= RG):
                        take_x((r + 2) % RG, n + 2)
                    take_h(r, n)

            for t0 in (0, PASS_TURNS):
                take_x(0, RG * t0)
                take_x(1, RG * t0 + 1)
                turn_of(t0)
                with act.Fori(t0 + 1, t0 + PASS_TURNS - 1) as i:
                    turn_of(i)
                turn_of(t0 + PASS_TURNS - 1, last=True)

        @block.vector
        def _(dve):
            def step(ins):
                steps[0] += 1
                ins.then_inc(table_step, 1)
                dve.wait_ge(table_step, steps[0])

            steps = [0]
            dve.memset(rows[:], 0.0).then_inc(cleared, 1)
            dve.wait_ge(const_in, 5 * 16)
            step(dve.tensor_tensor(tiles[:, :, :], fill[:, :, :], slot0[:, :, :], ALU.subtract))
            step(dve.tensor_scalar(tiles[:, :, :], tiles[:, :, :], P / 2 - 0.5, 1.0 / P, ALU.add, ALU.mult))
            step(dve.tensor_scalar(tiles[:, :, :], tiles[:, :, :], 2.0 ** 23, -2.0 ** 23, ALU.add, ALU.add))
            for k in range(2):
                ins = dve.tensor_tensor(part_sum[:, k, :, :], lower[:, :, :],
                                        tiles[:, k, :].unsqueeze(1).to_broadcast([P, EX, EX]), ALU.mult)
            step(ins)
            step(dve.tensor_reduce(ends[:, :, :], part_sum[:, :, :, :], mybir.AxisListType.X, ALU.add))
            for k in range(2):
                ins = dve.tensor_tensor(gone[:, k, :, :], ends[:, k, :].unsqueeze(1).to_broadcast([P, TP, EX]),
                                        tile_no[:, :].unsqueeze(2).to_broadcast([P, TP, EX]), ALU.is_le)
            step(ins)
            for k in range(2):
                ins = dve.tensor_tensor(gone_tiles[:, k, :, :], gone[:, k, :, :],
                                        tiles[:, k, :].unsqueeze(1).to_broadcast([P, TP, EX]), ALU.mult)
            step(ins)
            step(dve.tensor_reduce(expert[:, :, :], gone[:, :, :, :], mybir.AxisListType.X, ALU.add))
            step(dve.tensor_reduce(start[:, :, :], gone_tiles[:, :, :, :], mybir.AxisListType.X, ALU.add))
            step(dve.tensor_tensor(start[:, :, :], tile_base[:, :, :], start[:, :, :], ALU.subtract))
            flat_expert = expert[:, :, :].rearrange("p k t -> p (k t)")
            step(dve.tensor_scalar(expert_of[:, :], flat_expert, EX - 1.0, None, ALU.min))
            step(dve.tensor_scalar(flat_expert, flat_expert, float(CAP // P), None, ALU.mult))
            dve.tensor_tensor(list_tile[:, :], flat_expert, start[:, :, :].rearrange("p k t -> p (k t)"),
                              ALU.add).then_inc(table_ready, 1)
            dve.wait_ge(table_ready, 1)
            dve.wait_ge(w_in, 4 * 16)

            def expert_at(n):
                return dve.value_load(expert_of[0:1, bass.ds(n, 1)], min_val=0, max_val=EX - 1)

            def bias(r, n):
                e = expert_at(n)
                dve.wait_ge(h_ready, n + 1)
                if not isinstance(n, int) or n >= 2:
                    dve.wait_ge(hT_ready, n - 1)
                dve.tensor_tensor(hid[:, r % 2, :], ps_h[r % 2][:, :],
                                  b1[:, bass.ds(e, 1), :].rearrange("p o h -> p (o h)"), ALU.add).then_inc(biased, 1)

            def mix(r, n):
                e = expert_at(n)
                dve.wait_ge(y_ready, n + 1)
                if not isinstance(n, int) or n >= 1:
                    dve.wait_ge(mixed, n)
                dve.tensor_tensor(y[:, :], ps_y[r % 2][:, 0:D],
                                  b2[:, bass.ds(e, 1), :].rearrange("p o h -> p (o h)"), ALU.add).then_inc(y_taken, 1)
                dve.wait_ge(y_taken, n + 1)
                dve.scalar_tensor_tensor(out=rows[:, r, 1, :], in0=y[:, :], scalar=entry[:, r, 1:2],
                                         in1=rows[:, r, 1, :], op0=ALU.mult, op1=ALU.add).then_inc(mixed, 1)

            def turn_of(turn, first=False, last=False):
                for r in range(RG):
                    n = RG * turn + r
                    if not (last and r + 1 >= RG):
                        bias((r + 1) % RG, n + 1)
                    if not (first and r == 0):
                        mix((r - 1) % RG, n - 1)

            for t0 in (0, PASS_TURNS):
                bias(0, RG * t0)
                turn_of(t0, first=True)
                with dve.Fori(t0 + 1, t0 + PASS_TURNS - 1) as i:
                    turn_of(i)
                turn_of(t0 + PASS_TURNS - 1, last=True)
                mix(RG - 1, RG * (t0 + PASS_TURNS) - 1)


def build(nc, a, out):
    xy_dram = [nc.dram_tensor(f"xy_scratch{k}", [B * N, 2 * D], F32).ap() for k in range(2)]
    list_dram = nc.dram_tensor("list_scratch", [LIST_TILES * P, 2], F32).ap()
    with nc.sbuf_tensor("fill", [P, 2, EX], F32) as fill:
        attention_phase(nc, a, xy_dram[0], list_dram, fill)
        expert_phase(nc, a, xy_dram, list_dram, fill, out)


def kernel(**inputs):
    import numpy as np
    import concourse.bacc as bacc
    from concourse.bass_utils import run_bass_kernel_spmd

    g = {k: np.asarray(v) for k, v in inputs.items()}

    def rows(v):
        return np.ascontiguousarray(np.broadcast_to(v[None], (P,) + v.shape))

    arrays = {
        "x": g["x"], "adjT": np.ascontiguousarray(g["adj"].T),
        "WqT": np.ascontiguousarray(g["L0_gnn_Wq"].T), "WkT": np.ascontiguousarray(g["L0_gnn_Wk"].T),
        "WvT": np.ascontiguousarray(g["L0_gnn_Wv"].T), "WoT": np.ascontiguousarray(g["L0_gnn_Wo"].T),
        "bq": g["L0_gnn_bq"].reshape(P, 1), "bk": g["L0_gnn_bk"].reshape(P, 1),
        "bv": rows(g["L0_gnn_bv"]), "bo": rows(g["L0_gnn_bo"]),
        "gamma": rows(g["L0_gnn_gamma"]), "beta": rows(g["L0_gnn_beta"]),
        "Wg": g["L0_ffn_Wg"], "bg": rows(g["L0_ffn_bg"]),
        "W1": g["L0_ffn_W1"], "W2": g["L0_ffn_W2"],
        "b1": rows(g["L0_ffn_b1"]), "b2": rows(g["L0_ffn_b2"]),
        "ident": np.eye(P, dtype=np.float32), "iota": rows(np.arange(EX, dtype=np.float32)),
    }
    slot0 = np.array([[(k * PASS_TILES + e * CAP // P) * P for e in range(EX)] for k in range(2)], np.float32)
    pads = np.zeros((P, 2), np.float32)
    pads.view(np.int32)[:, 0] = B * N + np.arange(P)
    arrays |= {
        "earlier": np.triu(np.ones((P, P), np.float32), 1),
        "token_no": np.ascontiguousarray(np.arange(B * N, dtype=np.int32).reshape(B * T, P).T),
        "slot0": rows(slot0), "pads": rows(pads.reshape(-1)),
        "lower": rows(np.tril(np.ones((EX, EX), np.float32))), "tile_no": rows(np.arange(TP, dtype=np.float32)),
        "tile_base": rows(np.array([[k * PASS_TILES + i for i in range(TP)] for k in range(2)], np.float32)),
    }
    nc = bacc.Bacc("TRN2", target_bir_lowering=False, num_devices=1)
    a = {k: nc.dram_tensor(k + "_dram", v.shape, mybir.dt.from_np(v.dtype), kind="ExternalInput").ap()
         for k, v in arrays.items()}
    out = nc.dram_tensor("out", (B, N, D), F32, kind="ExternalOutput").ap()
    build(nc, a, out)
    r = run_bass_kernel_spmd(nc, [{k + "_dram": v for k, v in arrays.items()}], core_ids=[0])
    return r.results[0]["out"]
```

```python
import math
from contextlib import ExitStack

import concourse.bass as bass
from concourse import mybir

F32 = mybir.dt.float32
F32R = mybir.dt.float32r
BF16 = mybir.dt.bfloat16
I32 = mybir.dt.int32
U32 = mybir.dt.uint32
ALU = mybir.AluOpType
ACT = mybir.ActivationFunctionType

P = 128
B, N, D = 8, 1024, 128
H, DH = 4, 32
NC = N // P
T = N // P
NQ = 512
UNITS = (N // NQ) * NC
SLOTS = 2 * UNITS
EX, HID = 8, 512
HB = HID // P
EARLY = 2
CONSTS = 13
SCALE = float(DH) ** -0.5
CLIP = 10.0
EPS = 1e-5
RING = 4
CRING = 8
GROUP = 4
NG = UNITS // GROUP
Q_PARTS = (0, 1, 0, 1)
K_PARTS = (0, 0, 1, 1)
AHEAD, RG = 8, 12
CAP = B * N + P
TP = -(-(B * N // P + EX - 1) // RG) * RG
NT = 2 * TP
PASS_TILES = EX * CAP // P + TP
LIST_TILES = -(-2 * PASS_TILES // P) * P
PIECES = {0: ("cT", 0), 1: ("wo", 0), 2: ("xT", 0), 3: ("rank", 0), 4: ("xT", 1), 5: ("q", 0), 6: ("q", 1),
          7: ("v", 0), 8: ("cT", 1), 9: ("wo", 1), 10: ("k", 0), 11: ("k", 1), 12: ("v", 1), 13: ("yT", 0),
          14: ("yT", 1), 15: ("gate", 0)}
LISTING = (5, 6, 7, 8, 9, 13, 14, 15)
NEXT = ("xT", "q", "k", "v")


def attention_phase(nc, a, xy_dram, list_dram, expert_of, list_tile, ident, shared, weights, w_in):
    with ExitStack() as ctx:
        def sb(name, shape, dt=F32):
            return ctx.enter_context(nc.sbuf_tensor(name, shape, dt))

        def pb(name, shape, dt=F32):
            return ctx.enter_context(nc.psum_tensor(name, shape, dt))

        def sem(name):
            return ctx.enter_context(nc.semaphore(name))

        w_q, w_k, w_v, w_o = (sb(n, [P, D]) for n in ("w_q", "w_k", "w_v", "w_o"))
        w_g = sb("w_g", [P, EX])
        b_q, b_k = sb("b_q", [P, 1]), sb("b_k", [P, 1])
        b_v, b_o, gamma, beta = (sb(n, [P, D]) for n in ("b_v", "b_o", "gamma", "beta"))
        b_g, iota_e = sb("b_g", [P, EX]), sb("iota_e", [P, EX])
        place = sb("place", [P, GROUP, DH])
        minus_half = sb("minus_half", [P, T])
        earlier, every = sb("earlier", [P, P], BF16), sb("every", [P, P], BF16)
        token_no = sb("token_no", [P, B * T], I32)
        cap = shared["cap"]
        q_stack = [sb(f"q_stack{i}", [P, H, N], F32R) for i in range(2)]
        k_stack = [sb(f"k_stack{i}", [P, H, N], F32R) for i in range(2)]
        v_sb = [sb(f"v_sb{i}", [P, NC, D]) for i in range(2)]
        ctx_n = [sb(f"ctx_n{i}", [P, T, D]) for i in range(2)]
        xn_bo = [sb(f"xn_bo{i}", [P, T, D]) for i in range(2)]
        x_in, xn, x_res = shared["x_in"], sb("xn", [P, T, D]), sb("x_res", [P, T, D])
        xnT = sb("xnT", [P, N])
        part = [sb(f"part{i}", [P, N], F32R) for i in range(2)]
        full = shared["full"]
        g, yn, ynT = sb("g", [P, T, D]), sb("yn", [P, T, D]), sb("ynT", [P, N])
        st = sb("st", [P, T, 6])
        mv_x, mv_g, mv_y = (sb(n, [P, T, 2]) for n in ("mv_x", "mv_g", "mv_y"))
        rs_x, rs_g, rs_y = (sb(n, [P, T]) for n in ("rs_x", "rs_g", "rs_y"))
        off_x, off_g, off_y = (sb(n, [P, T]) for n in ("off_x", "off_g", "off_y"))
        logit, top, topi = sb("logit", [P, T, EX]), sb("top", [P, T, 8]), sb("topi", [P, T, 8], U32)
        topf = sb("topf", [P, T, 2])
        gap, egap = sb("gap", [P, T]), sb("egap", [P, T])
        hot = sb("hot", [P, T + 1, 2 * EX], BF16)
        pos, slot_f = sb("pos", [P, T, 2 * EX]), sb("slot_f", [P, T, 2])
        fill = sb("fill", [P, 2, EX])
        listing = [sb("listing0", [P, T, 2, 2]), shared["listing1"]]
        slot = [sb("slot0_sb", [P, T, 2], I32), shared["slot1"]]
        mark = sb("mark", [P, 2])
        probs = shared["probs"]
        ctx_sb = sb("ctx_sb", [P, CRING, NQ])
        den_sb = sb("den_sb", [P, NQ])
        recip = sb("recip", [P, 2, 4, H, GROUP])
        prod = sb("prod", [P, 2, 4, D])
        ctxT = ynT

        ps_s = [pb(f"ps_s{i}", [P, 2, NQ]) for i in range(2)]
        ps_c = pb("ps_c", [P, NQ])
        ps_d = pb("ps_d", [P, NQ])
        ps_t = pb("ps_t", [P, NQ])
        ps_x = pb("ps_x", [P, NQ])

        const_in = sem("const_in")
        adj_in = [sem(f"adj_in{i}") for i in range(2)]
        adj_hot, adj_read = sem("adj_hot"), sem("adj_read")
        cap_ready, place_ready = sem("cap_ready"), sem("place_ready")
        bias_ready = sem("bias_ready")
        x_loaded, res_loaded = sem("x_loaded"), sem("res_loaded")
        stats_x, rstd_x, xn_ready, xnbo_ready = sem("stats_x"), sem("rstd_x"), sem("xn_ready"), sem("xnbo_ready")
        xT_ready, xT_taken = sem("xT_ready"), sem("xT_taken")
        qk_ready, qk_taken, qk_high, qk_low = sem("qk_ready"), sem("qk_taken"), sem("qk_high"), sem("qk_low")
        v_ready, v_taken = sem("v_ready"), sem("v_taken")
        q_copied, stacked = sem("q_copied"), [sem(f"stacked{i}") for i in range(2)]
        scores_ready, clipped, probs_ready = sem("scores_ready"), sem("clipped"), sem("probs_ready")
        ctx_ready, den_ready = sem("ctx_ready"), sem("den_ready")
        ctx_taken, den_taken, denT_ready = sem("ctx_taken"), sem("den_taken"), sem("denT_ready")
        ctxT_ready, recip_ready, scaled, summed = sem("ctxT_ready"), sem("recip_ready"), sem("scaled"), sem("summed")
        cT_ready, cT_taken = sem("cT_ready"), sem("cT_taken")
        wo_ready, wo_taken = sem("wo_ready"), sem("wo_taken")
        stats_g, rstd_g, tn_ready, x2_ready = sem("stats_g"), sem("rstd_g"), sem("tn_ready"), sem("x2_ready")
        stats_y, rstd_y, yn_ready = sem("stats_y"), sem("rstd_y"), sem("yn_ready")
        yT_ready, yT_taken, gate_ready, gate_taken = sem("yT_ready"), sem("yT_taken"), sem("gate_ready"), sem("gate_taken")
        rank_ready, rank_taken = sem("rank_ready"), sem("rank_taken")
        gap_ready, egap_ready, hot_ready = sem("gap_ready"), sem("egap_ready"), sem("hot_ready")
        listing_ready, slots_ready = sem("listing_ready"), sem("slots_ready")
        listed = [sem(f"listed{i}") for i in range(2)]
        listing_free = sem("listing_free")
        x2_stored, yn_stored = sem("x2_stored"), sem("yn_stored")
        late_in = sem("late_in")
        first_high, first_low = sem("first_high"), sem("first_low")
        pads_in, lists_blank = sem("pads_in"), sem("lists_blank")
        table_in, table_ready = sem("table_in"), sem("table_ready")
        dve_step, pool_step = sem("dve_step"), sem("pool_step")

        x_v = a["x"].rearrange("b (t p) d -> b p t d", p=P)
        xy_v = xy_dram.rearrange("(b t p) d -> b p t d", p=P, t=T)
        adj_v = a["adjT"].rearrange("(j p) n -> j p n", p=P)
        adj_buf = [g[:, :, :].bitcast(I32), yn[:, :, :].bitcast(I32)]
        tile_no, tile_base, lower, slot0 = (dst for dst, _ in weights["table"])

        def spare(buf, at, *shape):
            size, names = math.prod(shape), "abc"[:len(shape)]
            flat = buf[:, :, :].rearrange("p t d -> p (t d)") if len(buf.shape) == 3 else buf[:, :]
            return flat[:, at:at + size].rearrange(f"p ({' '.join(names)}) -> p {' '.join(names)}",
                                                   **dict(zip(names, shape)))

        gone = [spare(buf, 0, TP, EX) for buf in (xn, xnT)]
        gone_tiles = [spare(buf, 0, TP, EX) for buf in (v_sb[0], ctx_n[0])]
        expert, start = spare(xn, TP * EX, 2, TP), spare(xn, TP * (EX + 2), 2, TP)
        part_sum = spare(xnT, TP * EX, 2, EX, EX)
        tiles, ends = (spare(v_sb[0], TP * EX + 2 * EX * n, 2, EX) for n in range(2))
        k_part0 = [c[:, :, :].rearrange("p t d -> p (t d)").bitcast(F32R) for c in ctx_n]
        hot_buf = [x_res[:, :, :], ynT[:, :].rearrange("p (t d) -> p t d", t=T)]

        def wait_apart(eng, s, count):
            if not isinstance(count, int):
                count = eng.snap(count)
                eng.compute_val(count)
            eng.wait_ge(const_in, CONSTS * 16)
            eng.wait_ge(s, count)

        def before(b, s, lag):
            return (b, s - lag) if s >= lag else (b - 1, s - lag + UNITS)

        def lagged(b, s, lag, first, tail):
            return not (first and s < lag) and not (tail and s >= lag)

        def bodies(eng, body, chained=None, steps=0):
            body(0, 0, first=True)
            body(1, 1)
            body(2, 0)
            base = chained[1] if chained else 0
            with eng.Fori(1, (B - 2) // 2) as i:
                pair[0] = i
                if chained:
                    chained[0], chained[1] = i * steps + (base - steps), 0
                body(2 * i + 1, 1)
                body(2 * i + 2, 0)
                assert not chained or chained[1] == steps, chained[1]
            if chained:
                chained[0], chained[1] = base + (B - 4) // 2 * steps, 0
            body(B - 1, 1, last=True)
            body(B, 0, tail=True)

        def runs(kind, b, first=False, last=False, tail=False):
            if kind == "rank":
                return has(b, 2)
            return not (last or tail) if kind in NEXT else not first

        def has(b, n):
            return not isinstance(b, int) or b >= n

        pair = [None]

        def turn(b, par):
            return b // 2 if isinstance(b, int) else pair[0] + (par == 0)

        def start_bank(kind, half):
            return {"xT": (ps_x, ps_t), "v": (ps_c, ps_d), "q": (ps_s[0][:, 0, :], ps_s[0][:, 1, :]),
                    "k": (ps_s[1][:, 0, :], ps_s[1][:, 1, :])}[kind][half]

        def keys_stacked(b, par):
            if isinstance(b, int) and b == 0:
                return ((first_high, 128), (first_low, 128))
            return ((stacked[par], 256 * (turn(b, par) + par)),)

        block = ctx.enter_context(nc.Block())

        CONST_SP = [(ident, "ident"), (w_q, "WqT"), (w_k, "WkT"), (b_q, "bq"), (b_k, "bk"), (full[:, 0, 0:P], "earlier"),
                    (w_v, "WvT"), (b_v, "bv"), (b_o, "bo")]
        CONST_ACT = [(w_o, "WoT"), (w_g, "Wg"), (gamma, "gamma"), (beta, "beta")]
        CONST_LATE = [(b_g, "bg"), (iota_e, "iota"), (token_no, "token_no"), (fill, "slot0")]
        assert len(CONST_SP) + len(CONST_ACT) == CONSTS

        def stack(queue, par, which, b, rows=range(4), done=None):
            stacks, order = ((q_stack, Q_PARTS), (k_stack, K_PARTS))[which]
            parts = k_part0 if which and isinstance(b, int) and b == 0 else [p[:, :] for p in part]
            queue.wait_ge(qk_high, 4 * b + 2 * which + 2)
            queue.wait_ge(qk_low, 4 * b + 2 * which + 2)
            for row in rows:
                for h in range(H):
                    queue.dma_start(stacks[par][DH * row:DH * (row + 1), h, :].bitcast(F32),
                                 parts[order[row]][DH * h:DH * (h + 1), :].bitcast(F32))\
                        .then_inc(done or (stacked[par] if which else q_copied), 16)

        @block.sync
        def _(sp):
            def load_x(b):
                sp.dma_start(x_in[:, :, :], x_v[b]).then_inc(x_loaded, 16)

            def load_res(b):
                sp.dma_start(x_res[:, :, :], x_v[b]).then_inc(res_loaded, 16)

            def load_adj(j):
                sp.wait_ge(adj_hot, j - 1)
                sp.dma_start(adj_buf[j % 2], adj_v[j].rearrange("p (t d) -> p t d", t=T)).then_inc(adj_in[j % 2], 16)

            load_x(0)
            for dst, name in CONST_SP:
                sp.dma_start(dst[:], a[name]).then_inc(const_in, 16)
            for j in range(2, NC):
                load_adj(j)
            sp.wait_ge(xn_ready, 2)
            load_x(1)
            stack(sp, 0, 0, 0)
            stack(sp, 0, 1, 0, (0, 1), first_high)
            for dst, name in CONST_LATE:
                sp.dma_start(dst[:], a[name]).then_inc(late_in, 16)
            sp.dma_start(den_sb[:, 0:2 * P], a["pads"]).then_inc(pads_in, 16)
            sp.wait_ge(pads_in, 16)
            sp.dma_start(list_dram.rearrange("(p n q) c -> p n (q c)", p=P, q=P),
                         den_sb[:, 0:2 * P].unsqueeze(1).to_broadcast([P, LIST_TILES // P, 2 * P]))\
                .then_inc(lists_blank, 16)
            sp.wait_ge(cap_ready, NC)
            load_res(0)

            def store(b):
                sp.wait_ge(yn_ready, 2 * b + 2)
                sp.dma_start(xy_v[b][:, :, D:], g[:, :, :]).then_inc(x2_stored, 16)
                sp.dma_start(xy_v[b][:, :, 0:D], yn[:, :, :]).then_inc(yn_stored, 16)

            def body(b, par, first=False, last=False):
                if not last:
                    if not first:
                        sp.wait_ge(scores_ready, SLOTS * b)
                    stack(sp, 1 - par, 0, b + 1)
                    stack(sp, 1 - par, 1, b + 1)
                if not first:
                    store(b - 1)
                    load_res(b)

            def whole(b, par, first=False):
                sp.wait_ge(xn_ready, 2 * b + 4)
                load_x(b + 2)
                body(b, par, first)

            whole(0, 0, first=True)
            with sp.Fori(0, (B - 4) // 2) as i:
                whole(2 * i + 1, 1)
                whole(2 * i + 2, 0)
            whole(B - 3, 1)
            body(B - 2, 0)
            body(B - 1, 1, last=True)
            sp.wait_ge(xn_ready, 2 * B)
            sp.wait_ge(qk_low, 4 * B)
            for dst, name in weights["table"]:
                sp.dma_start(dst, a[name]).then_inc(table_in, 16)
            for dst, name in weights["input"]:
                sp.dma_start(dst, a[name]).then_inc(w_in, 16)
            sp.wait_ge(clipped, SLOTS * B)
            for dst, name in weights["cap"]:
                sp.dma_start(dst, a[name]).then_inc(w_in, 16)
            sp.wait_ge(den_ready, UNITS * B)
            for dst, name in weights["probs"]:
                sp.dma_start(dst, a[name]).then_inc(w_in, 16)
            store(B - 1)
            sp.wait_ge(x2_stored, 16 * B)
            sp.wait_ge(yn_stored, 16 * B)

        @block.tensor
        def _(pe):
            def spare_free(b, s, *which):
                before_ = [k for k in sorted(PIECES) if k < s and runs(PIECES[k][0], b, *which)]
                if before_:
                    taken(*PIECES[before_[-1]], b)
                else:
                    pe.wait_ge(v_taken, 2 * min(b, B - 1) + 2 if isinstance(b, int) else 2 * b + 2)
                    if not (isinstance(b, int) and b == 0):
                        pe.wait_ge(gate_taken, b)

            def taken(kind, half, b):
                sem_, count = {"xT": (xT_taken, 2 * (b + 1)), "wo": (wo_taken, 2 * (b - 1)),
                               "cT": (cT_taken, 2 * (b - 1)),
                               "q": (qk_taken, 4 * (b + 1)), "k": (qk_taken, 4 * (b + 1) + 2),
                               "v": (v_taken, 2 * (b + 1)), "yT": (yT_taken, 2 * (b - 1)),
                               "rank": (rank_taken, b - 2) if has(b, 2) else None,
                               "gate": (gate_taken, b)}[kind]
                pe.wait_ge(sem_, count + half + 1)

            def piece(kind, half, b, par, ps_x=ps_x):
                lo = half * NQ
                if kind == "xT":
                    pe.wait_ge(xn_ready, 2 * b + half + 1)
                    for t in range(4):
                        last = pe.transpose(ps_x[:, t * P:(t + 1) * P], xn[:, 4 * half + t, :], ident[:, :])
                    last.then_inc(xT_ready, 1)
                elif kind in "qk":
                    pe.wait_ge(xT_taken, 2 * b + half + 1)
                    w = w_q if kind == "q" else w_k
                    pe.matmul(ps_x[:, :], w[:, :], xnT[:, lo:lo + NQ], start=True, stop=True).then_inc(qk_ready, 1)
                elif kind == "v":
                    for t in range(4):
                        last = pe.matmul(ps_x[:, t * P:(t + 1) * P], xnT[:, lo + t * P:lo + (t + 1) * P], w_v[:, :],
                                         start=True, stop=True)
                    last.then_inc(v_ready, 1)
                elif kind == "cT":
                    pe.wait_ge(summed, 14 * b + 7 * (half + 1))
                    for t in range(4):
                        last = pe.transpose(ps_x[:, t * P:(t + 1) * P], ctx_n[par][:, 4 * half + t, :], ident[:, :])
                    last.then_inc(cT_ready, 1)
                elif kind == "wo":
                    pe.wait_ge(cT_taken, 2 * b + half + 1)
                    for t in range(4):
                        last = pe.matmul(ps_x[:, t * P:(t + 1) * P], ctxT[:, lo + t * P:lo + (t + 1) * P], w_o[:, :],
                                         start=True, stop=True)
                    last.then_inc(wo_ready, 1)
                elif kind == "yT":
                    pe.wait_ge(yn_ready, 2 * b + half + 1)
                    for t in range(4):
                        last = pe.transpose(ps_x[:, t * P:(t + 1) * P], yn[:, 4 * half + t, :], ident[:, :])
                    last.then_inc(yT_ready, 1)
                else:
                    pe.wait_ge(yT_taken, 2 * b + 2)
                    for t in range(T):
                        last = pe.matmul(ps_x[:, t * EX:(t + 1) * EX], ynT[:, t * P:(t + 1) * P], w_g[:, :],
                                         start=True, stop=True)
                    last.then_inc(gate_ready, 1)

            def ranks(b):
                rank = ps_x[:, 0:(T + 1) * 2 * EX].rearrange("p (t c) -> p t c", c=2 * EX)
                pe.wait_ge(hot_ready, b + 1)
                pe.matmul(rank, earlier[:, :], hot[:, :, :], start=True, stop=False)
                for t in range(T):
                    last = pe.matmul(rank[:, t + 1:, :], every[:, :],
                                     hot[:, t:t + 1, :].to_broadcast([P, T - t, 2 * EX]), start=False, stop=(t == T - 1))
                last.then_inc(rank_ready, 1)

            def scores(b, par, u, hp):
                half, j = divmod(u, NC)
                slot = 2 * u + hp
                if not (isinstance(b, int) and b == 0 and slot < 2):
                    pe.wait_ge(clipped, SLOTS * b + slot - 1)
                for n in range(2):
                    h = 2 * hp + n
                    last = pe.matmul(ps_s[hp][:, n, :], k_stack[par][:, h, j * P:(j + 1) * P],
                                     q_stack[par][:, h, half * NQ:(half + 1) * NQ], start=True, stop=True)
                last.then_inc(scores_ready, 1)

            def context(b, par, u):
                j = u % NC
                pe.wait_ge(probs_ready, SLOTS * b + 2 * u + 2)
                if not (isinstance(b, int) and b == 0 and u < 1):
                    pe.wait_ge(ctx_taken, UNITS * b + u)
                for h in range(H):
                    last = pe.matmul(ps_c[DH * h:DH * (h + 1), :], v_sb[par][:, j, DH * h:DH * (h + 1)],
                                     probs[:, u % RING, h, :], start=True, stop=True, tile_position=(0, DH * h))
                last.then_inc(ctx_ready, 1)

            def denominators(b, u):
                g_ = u % GROUP
                if g_ == 0 and not (isinstance(b, int) and b == 0 and u < GROUP):
                    pe.wait_ge(den_taken, NG * b + u // GROUP)
                for h in range(H):
                    last = pe.matmul(ps_d[DH * h:DH * (h + 1), :], place[:, g_, :], probs[:, u % RING, h, :],
                                     start=(g_ == 0), stop=(g_ == GROUP - 1), tile_position=(0, DH * h))
                last.then_inc(den_ready, 1)

            def transpose_den(b, group):
                pe.wait_ge(den_taken, NG * b + group + 1)
                if not (isinstance(b, int) and b == 0 and group == 0):
                    pe.wait_ge(scaled, UNITS * b + GROUP * group)
                for t in range(4):
                    last = pe.transpose(ps_t[:, t * P:(t + 1) * P], den_sb[:, t * P:(t + 1) * P], ident[:, :])
                last.then_inc(denT_ready, 1)

            def transpose_ctx(b, u):
                pe.wait_ge(ctx_taken, UNITS * b + u + 1)
                pe.wait_ge(recip_ready, NG * b + u // GROUP + 1)
                if u % GROUP:
                    pe.wait_ge(scaled, UNITS * b + u)
                for t in range(4):
                    last = pe.transpose(ps_t[:, t * P:(t + 1) * P], ctx_sb[:, u % CRING, t * P:(t + 1) * P], ident[:, :])
                last.then_inc(ctxT_ready, 1)

            def body(b, par, first=False, last=False, tail=False):
                if not tail:
                    pe.wait_ge(q_copied, 256 * (b + 1))
                    for done, count in keys_stacked(b, par):
                        pe.wait_ge(done, count)
                    pe.wait_ge(v_taken, 2 * b + 2)
                for s in range(UNITS):
                    bb, u = before(b, s, 2)
                    if not tail:
                        scores(b, par, s, 0)
                    if not tail:
                        scores(b, par, s, 1)
                    if lagged(b, s, 2, first, tail):
                        context(bb, par if s >= 2 else 1 - par, u)
                    if lagged(b, s, 2, first, tail):
                        denominators(bb, u)
                    if s % GROUP == 3 and lagged(b, s, 7, first, tail):
                        transpose_den(before(b, s, 7)[0], before(b, s, 7)[1] // GROUP)
                    if s % GROUP != 3 and lagged(b, s, 7, first, tail):
                        transpose_ctx(*before(b, s, 7))
                    if s in PIECES:
                        kind, half = PIECES[s]
                        if runs(kind, b, first, last, tail):
                            spare_free(b, s, first, last, tail)
                            if kind == "rank":
                                ranks(b - 2)
                            else:
                                piece(kind, half, b + 1 if kind in NEXT else b - 1, 1 - par)
                    if s % GROUP == 3 and lagged(b, s, 7, first, tail):
                        transpose_ctx(*before(b, s, 7))

            pe.wait_ge(const_in, CONSTS * 16)
            for kind in ("xT", "q", "k", "v"):
                for half in range(2):
                    piece(kind, half, 0, 0, start_bank(kind, half))
            pe.wait_ge(place_ready, 1)
            bodies(pe, body)
            pe.wait_ge(gate_taken, B + 1)
            ranks(B - 1)

        @block.scalar
        def _(act):
            def probabilities(b, u, pair):
                act.wait_ge(clipped, SLOTS * b + 2 * u + pair + 1)
                buf = probs[:, u % RING, 2 * pair:2 * pair + 2, :]
                act.activation(buf, buf, ACT.Exp).then_inc(probs_ready, 1)

            def take_context(b, u):
                act.wait_ge(ctx_ready, UNITS * b + u + 1)
                if not (isinstance(b, int) and b == 0 and u < CRING):
                    act.wait_ge(ctxT_ready, UNITS * b + u - CRING + 1)
                act.activation(ctx_sb[:, u % CRING, :], ps_c[:, :], ACT.Copy).then_inc(ctx_taken, 1)

            def take_den(b, group):
                act.wait_ge(den_ready, UNITS * b + GROUP * (group + 1))
                if isinstance(b, int) and b == 0 and group == 0:
                    act.wait_ge(lists_blank, 16)
                else:
                    act.wait_ge(denT_ready, NG * b + group)
                act.activation(den_sb[:, :], ps_d[:, :], ACT.Copy).then_inc(den_taken, 1)

            def take(kind, half, b, ps_x=ps_x, part=part, parts_copied=()):
                lo = half * NQ
                if kind == "xT":
                    act.wait_ge(xT_ready, 2 * b + half + 1)
                    act.activation(xnT[:, lo:lo + NQ], ps_x[:, :], ACT.Copy).then_inc(xT_taken, 1)
                elif kind in ("q", "k"):
                    n = 4 * b + 2 * (kind == "k") + half
                    act.wait_ge(qk_ready, n + 1)
                    if not (isinstance(b, int) and b == 0 and kind == "q"):
                        act.wait_ge(qk_low, n - 1)
                    act.activation(full[:, half, :], ps_x[:, :], ACT.Identity, bias=(b_q if kind == "q" else b_k)[:, :],
                                   scale=SCALE if kind == "q" else 1.0).then_inc(qk_taken, 1)
                    act.wait_ge(qk_taken, n + 1)
                    for done, count in parts_copied:
                        act.wait_ge(done, count)
                    act.activation(part[0][:, lo:lo + NQ], full[:, half, :], ACT.Copy).then_inc(qk_high, 1)
                elif kind == "cT":
                    act.wait_ge(cT_ready, 2 * b + half + 1)
                    if not (isinstance(b, int) and b == 0):
                        act.wait_ge(gate_ready, b)
                    act.activation(ctxT[:, lo:lo + NQ], ps_x[:, :], ACT.Copy).then_inc(cT_taken, 1)
                elif kind == "yT":
                    act.wait_ge(yT_ready, 2 * b + half + 1)
                    act.activation(ynT[:, lo:lo + NQ], ps_x[:, :], ACT.Copy).then_inc(yT_taken, 1)

            def normalise(dst, src, rs, off, done):
                for t in range(src.shape[1]):
                    ins = act.activation(dst[:, t, :], src[:, t, :], ACT.Identity, bias=off[:, t:t + 1],
                                         scale=rs[:, t:t + 1])
                ins.then_inc(done, 1)

            def norm_of_x(b, half):
                act.wait_ge(rstd_x, b + 1)
                if not (isinstance(b, int) and b == 0):
                    act.wait_ge(xnbo_ready, b)
                t = slice(4 * half, 4 * half + 4)
                normalise(xn[:, t, :], x_in[:, t, :], rs_x[:, t], off_x[:, t], xn_ready)

            def norm_of_g(b, half):
                act.wait_ge(rstd_g, 2 * b + half + 1)
                t = slice(4 * half, 4 * half + 4)
                normalise(g[:, t, :], g[:, t, :], rs_g[:, t], off_g[:, t], tn_ready)

            def norm_of_y(b, half):
                act.wait_ge(rstd_y, 2 * b + half + 1)
                if not (isinstance(b, int) and b == 0):
                    act.wait_ge(yT_ready, 2 * b)
                    act.wait_ge(yn_stored, 16 * b)
                t = slice(4 * half, 4 * half + 4)
                normalise(yn[:, t, :], g[:, t, :], rs_y[:, t], off_y[:, t], yn_ready)

            def gap_exp(b):
                act.wait_ge(gap_ready, b + 1)
                act.activation(egap[:, :], gap[:, :], ACT.Exp).then_inc(egap_ready, 1)

            def body(b, par, first=False, last=False, tail=False):
                for s in range(UNITS):
                    if s % GROUP == 2 and lagged(b, s, 6, first, tail):
                        take_den(before(b, s, 6)[0], before(b, s, 6)[1] // GROUP)
                    if s - 1 in PIECES:
                        kind, half = PIECES[s - 1]
                        if runs(kind, b, first, last, tail):
                            parts_copied = ((q_copied, 256 * (b + 2)),) if kind == "k" else keys_stacked(b, par)
                            take(kind, half, b + 1 if kind in NEXT else b - 1, parts_copied=parts_copied)
                    if lagged(b, s, 2, first, tail):
                        take_context(*before(b, s, 2))
                    if not tail:
                        probabilities(b, s, 0)
                    if not first and s in (6, 14):
                        norm_of_y(b - 1, s // 8)
                    if not tail:
                        probabilities(b, s, 1)
                    if runs("xT", b, first, last, tail) and s in (1, 2):
                        norm_of_x(b + 1, s - 1)
                    if not first:
                        for half, at in enumerate((2, 10)):
                            if s == at + 1:
                                norm_of_g(b - 1, half)
                    if s == 2 and has(b, 2):
                        gap_exp(b - 2)

            def make_cap(j):
                act.wait_ge(adj_hot, j + 1)
                act.activation(cap[:, j, :].rearrange("p (t d) -> p t d", t=T), hot_buf[j % 2], ACT.Copy,
                               bias=-CLIP, scale=2 * CLIP).then_inc(cap_ready, 1)

            for j in range(2):
                act.dma_start(adj_buf[j], adj_v[j].rearrange("p (t d) -> p t d", t=T)).then_inc(adj_in[j], 16)
            for dst, name in CONST_ACT:
                act.dma_start(dst[:], a[name]).then_inc(const_in, 16)
            for j in range(EARLY):
                make_cap(j)
            act.wait_ge(bias_ready, 1)
            for half in range(2):
                norm_of_x(0, half)
            for half in range(2):
                take("xT", half, 0, start_bank("xT", half))
            for half in range(2):
                take("q", half, 0, start_bank("q", half))
            for j in range(EARLY, EARLY + 2):
                make_cap(j)
            for half in range(2):
                take("k", half, 0, start_bank("k", half), k_part0)
            for j in range(EARLY + 2, NC):
                make_cap(j)
            bodies(act, body)
            gap_exp(B - 1)

        @block.vector
        def _(dve):
            chained = [0, 0]

            def step(ins):
                chained[1] += 1
                ins.then_inc(dve_step, 1)
                dve.wait_ge(dve_step, chained[0] + chained[1])

            def plain_step(ins):
                chained[1] += 1
                ins.then_inc(dve_step, 1)
                wait_apart(dve, dve_step, chained[0] + chained[1])

            def clip(b, u, hp):
                half, j = divmod(u, NC)
                dve.wait_ge(scores_ready, SLOTS * b + 2 * u + hp + 1)
                if isinstance(b, int) and b == 0 and half == 0:
                    dve.wait_ge(cap_ready, j + 1)
                if not (isinstance(b, int) and b == 0 and u < RING):
                    dve.wait_ge(den_ready, UNITS * b + u - RING + 1)
                c = cap[:, j, half * NQ:(half + 1) * NQ].unsqueeze(1).to_broadcast([P, 2, NQ])
                dve.scalar_tensor_tensor(out=probs[:, u % RING, 2 * hp:2 * hp + 2, :], in0=ps_s[hp][:, :, :],
                                         scalar=-CLIP, in1=c, op0=ALU.max, op1=ALU.min).then_inc(clipped, 1)

            def invert(b, group):
                dve.wait_ge(denT_ready, NG * b + group + 1)
                den = ps_t[:, :].rearrange("p (t h g r) -> p t h g r", t=4, h=H, g=GROUP)[:, :, :, :, 0]
                dve.reciprocal(recip[:, group % 2, :, :, :], den).then_inc(recip_ready, 1)

            def scale(b, par, u):
                half, j = divmod(u, NC)
                group, g_ = divmod(u, GROUP)
                dve.wait_ge(recip_ready, NG * b + group + 1)
                dve.wait_ge(ctxT_ready, UNITS * b + u + 1)
                dst = ctx_n[par][:, 4 * half:4 * half + 4, :] if j == 0 else prod[:, u % 2, :, :]
                if j >= 3 or (j in (1, 2) and half == 1):
                    n = 7 * half + j - 2 if j >= 3 else 7
                    dve.wait_ge(summed, 14 * b + n)
                elif j in (1, 2) and not (isinstance(b, int) and b == 0):
                    dve.wait_ge(summed, 14 * b)
                r = recip[:, group % 2, :, :, g_].rearrange("p t h -> p (t h)").unsqueeze(2).to_broadcast([P, 4 * H, DH])
                dve.tensor_tensor(dst.rearrange("p t (h d) -> p (t h) d", d=DH), ps_t[:, :].rearrange("p (t d) -> p t d", d=DH),
                                  r, ALU.mult).then_inc(scaled, 1)

            def statistics(src, st, mv, done):
                for t in range(src.shape[1]):
                    ins = dve.bn_stats(st[:, t, :], src[:, t, :])
                plain_step(ins)
                for t in range(src.shape[1]):
                    ins = dve.bn_aggr(mv[:, t, :], st[:, t, :])
                ins.then_inc(done, 1)

            def stats_of_x(b):
                dve.wait_ge(x_loaded, 16 * (b + 1))
                statistics(x_in, st, mv_x, stats_x)

            def take(kind, half, b, par, ps_x=ps_x):
                if kind == "v":
                    dve.wait_ge(v_ready, 2 * b + half + 1)
                    dst = v_sb[par][:, 4 * half:4 * half + 4, :]
                    dve.tensor_tensor(dst, ps_x[:, :].rearrange("p (t d) -> p t d", t=4),
                                      b_v[:, :].unsqueeze(1).to_broadcast([P, 4, D]), ALU.add).then_inc(v_taken, 1)
                elif kind == "wo":
                    dve.wait_ge(wo_ready, 2 * b + half + 1)
                    dve.wait_ge(xnbo_ready, b + 1)
                    if not (isinstance(b, int) and b == 0):
                        dve.wait_ge(x2_stored, 16 * b)
                    dve.tensor_tensor(g[:, 4 * half:4 * half + 4, :], ps_x[:, :].rearrange("p (t d) -> p t d", t=4),
                                      xn_bo[par][:, 4 * half:4 * half + 4, :], ALU.add).then_inc(wo_taken, 1)
                elif kind == "rank":
                    take_ranks(b - 1)
                elif kind == "gate":
                    dve.wait_ge(gate_ready, b + 1)
                    dve.tensor_tensor(logit[:, :, :], ps_x[:, 0:T * EX].rearrange("p (t e) -> p t e", e=EX),
                                      b_g[:, :].unsqueeze(1).to_broadcast([P, T, EX]), ALU.add).then_inc(gate_taken, 1)

            def choose(b):
                wait_apart(dve, gate_taken, b + 2)
                for t in range(T):
                    ins = dve.max(top[:, t, :], logit[:, t, :])
                plain_step(ins)
                for t in range(T):
                    ins = dve.max_index(topi[:, t, :], top[:, t, :], logit[:, t, :])
                step(ins)
                dve.tensor_tensor(gap[:, :], top[:, :, 1], top[:, :, 0], ALU.subtract).then_inc(gap_ready, 1)
                step(dve.tensor_copy(topf[:, :, :], topi[:, :, 0:2]))
                if has(b, 1):
                    dve.wait_ge(slots_ready, b)
                for k in range(2):
                    ins = dve.tensor_tensor(hot[:, 0:T, k * EX:(k + 1) * EX],
                                            iota_e[:, :].unsqueeze(1).to_broadcast([P, T, EX]),
                                            topf[:, :, k:k + 1].to_broadcast([P, T, EX]), ALU.is_equal)
                ins.then_inc(hot_ready, 1)

            def entries(b, par):
                entry = listing[par]
                dve.wait_ge(egap_ready, b + 1)
                dve.wait_ge(listing_free, b + 1)
                step(dve.tensor_scalar(entry[:, :, 1, 1], egap[:, :], 1.0, None, ALU.add))
                step(dve.reciprocal(entry[:, :, 0, 1], entry[:, :, 1, 1]))
                dve.tensor_tensor(entry[:, :, 1, 1], egap[:, :], entry[:, :, 0, 1], ALU.mult)
                dve.tensor_copy(entry[:, :, :, 0].bitcast(I32),
                                token_no[:, bass.ds(b * T, T)].unsqueeze(2).to_broadcast([P, T, 2]))\
                    .then_inc(listing_ready, 1)

            def take_ranks(b):
                dve.wait_ge(rank_ready, b + 1)
                rank = ps_x[:, 0:(T + 1) * 2 * EX].rearrange("p (t c) -> p t c", c=2 * EX)
                flat_fill = fill[:, :, :].rearrange("p k e -> p (k e)")
                if has(b, 1):
                    dve.wait_ge(rank_taken, b)
                step(dve.tensor_tensor(pos[:, :, :], rank[:, 0:T, :],
                                       flat_fill.unsqueeze(1).to_broadcast([P, T, 2 * EX]), ALU.add))
                dve.tensor_tensor(flat_fill, flat_fill, rank[:, T, :], ALU.add).then_inc(rank_taken, 1)

            def slots(b, par):
                step(dve.tensor_tensor(pos[:, :, :], pos[:, :, :], hot[:, 0:T, :], ALU.mult))
                step(dve.tensor_reduce(slot_f[:, :, :], pos[:, :, :].rearrange("p t (k e) -> p t k e", k=2),
                                       mybir.AxisListType.X, ALU.add))
                dve.tensor_copy(slot[par][:, :, :], slot_f[:, :, :]).then_inc(slots_ready, 1)

            def halves(half):
                return slice(4 * half, 4 * half + 4)

            def stats_of_g(b, half):
                dve.wait_ge(wo_taken, 2 * b + half + 1)
                statistics(g[:, halves(half), :], st[:, halves(half), :], mv_g[:, halves(half), :], stats_g)

            def stats_of_y(b, half):
                dve.wait_ge(x2_ready, 2 * b + half + 1)
                statistics(g[:, halves(half), :], st[:, halves(half), :], mv_y[:, halves(half), :], stats_y)

            def body(b, par, first=False, last=False, tail=False):
                for s in range(UNITS):
                    if lagged(b, s, 8, first, tail):
                        scale(before(b, s, 8)[0], par if s >= 8 else 1 - par, before(b, s, 8)[1])
                    if not tail:
                        clip(b, s, 0)
                    if s - 1 in PIECES:
                        kind, half = PIECES[s - 1]
                        if runs(kind, b, first, last, tail) and kind in ("v", "wo", "rank"):
                            take(kind, half, b + 1 if kind in NEXT else b - 1, 1 - par)
                    if s == 0 and has(b, 2):
                        take("gate", 0, b - 2, par)
                    if not first and s in (5, 13):
                        stats_of_y(b - 1, s // 8)
                    if not tail:
                        clip(b, s, 1)
                    if s % GROUP == 3 and lagged(b, s, 7, first, tail):
                        invert(before(b, s, 7)[0], before(b, s, 7)[1] // GROUP)
                    if runs("xT", b, first, last, tail) and s == 0:
                        stats_of_x(b + 1)
                    if not first:
                        for half, at in enumerate((2, 10)):
                            if s == at:
                                stats_of_g(b - 1, half)
                    if has(b, 2):
                        if s == 1:
                            choose(b - 2)
                        if s == 3:
                            entries(b - 2, par)
                        if s == 4:
                            slots(b - 2, par)

            def find_edges(j):
                dve.wait_ge(adj_in[j % 2], 16 * (j // 2 + 1))
                if j >= 2:
                    dve.wait_ge(cap_ready, j - 1)
                dve.tensor_scalar(hot_buf[j % 2], adj_buf[j % 2], 0.0, None, ALU.not_equal).then_inc(adj_hot, 1)

            for j in range(EARLY):
                find_edges(j)
            dve.wait_ge(const_in, CONSTS * 16)
            dve.tensor_copy(earlier[:, :], full[:, 0, 0:P])
            dve.tensor_scalar(b_q[:, :], b_q[:, :], SCALE, None, ALU.mult).then_inc(bias_ready, 1)
            dve.memset(every[:, :], 1.0)
            dve.memset(hot[:, T, :], 0.0)
            step(dve.memset(place[:, :, :], 0.0))
            for g_ in range(GROUP):
                ins = dve.memset(place[:, g_, DH // GROUP * g_:DH // GROUP * (g_ + 1)], 1.0)
            ins.then_inc(place_ready, 1)
            dve.memset(gap[:, :], 0.0).then_inc(gate_taken, 1)
            stats_of_x(0)
            for j in range(EARLY, NC):
                find_edges(j)
            for half in range(2):
                take("v", half, 0, 0, start_bank("v", half))
            dve.wait_ge(late_in, 16 * len(CONST_LATE))
            bodies(dve, body, chained, DVE_STEPS)
            take("gate", 0, B - 1, 1)
            choose(B - 1)
            entries(B - 1, 1)
            take_ranks(B - 1)
            slots(B - 1, 1)
            dve.wait_ge(slots_ready, B)
            dve.wait_ge(rank_taken, B)
            dve.wait_ge(table_in, 16 * len(weights["table"]))
            step(dve.tensor_tensor(tiles[:, :, :], fill[:, :, :], slot0, ALU.subtract))
            step(dve.tensor_scalar(tiles[:, :, :], tiles[:, :, :], P / 2 - 0.5, 1.0 / P, ALU.add, ALU.mult))
            step(dve.tensor_scalar(tiles[:, :, :], tiles[:, :, :], 2.0 ** 23, -2.0 ** 23, ALU.add, ALU.add))
            for k in range(2):
                ins = dve.tensor_tensor(part_sum[:, k, :, :], lower,
                                        tiles[:, k, :].unsqueeze(1).to_broadcast([P, EX, EX]), ALU.mult)
            step(ins)
            step(dve.tensor_reduce(ends[:, :, :], part_sum[:, :, :, :], mybir.AxisListType.X, ALU.add))
            for k in range(2):
                ins = dve.tensor_tensor(gone[k], ends[:, k, :].unsqueeze(1).to_broadcast([P, TP, EX]),
                                        tile_no.unsqueeze(2).to_broadcast([P, TP, EX]), ALU.is_le)
            step(ins)
            for k in range(2):
                ins = dve.tensor_tensor(gone_tiles[k], gone[k],
                                        tiles[:, k, :].unsqueeze(1).to_broadcast([P, TP, EX]), ALU.mult)
            step(ins)
            for k in range(2):
                ins = dve.tensor_reduce(expert[:, k, :], gone[k], mybir.AxisListType.X, ALU.add)
            step(ins)
            for k in range(2):
                ins = dve.tensor_reduce(start[:, k, :], gone_tiles[k], mybir.AxisListType.X, ALU.add)
            step(ins)
            step(dve.tensor_tensor(start[:, :, :], tile_base, start[:, :, :], ALU.subtract))
            flat_expert = expert[:, :, :].rearrange("p k t -> p (k t)")
            step(dve.tensor_scalar(expert_of[:, :], flat_expert, EX - 1.0, None, ALU.min))
            step(dve.tensor_scalar(flat_expert, flat_expert, float(CAP // P), None, ALU.mult))
            dve.tensor_tensor(list_tile[:, :], flat_expert, start[:, :, :].rearrange("p k t -> p (k t)"),
                              ALU.add).then_inc(table_ready, 1)

        @block.gpsimd
        def _(pool):
            chained = [0, 0]

            def step(ins):
                chained[1] += 1
                ins.then_inc(pool_step, 1)
                pool.wait_ge(pool_step, chained[0] + chained[1])

            def rstd(rs, off, mv, stats, done, count):
                wait_apart(pool, stats, count)
                pool.tensor_scalar(off, mv[:, :, 0], -1.0, None, ALU.mult)
                step(pool.tensor_scalar(rs, mv[:, :, 1], EPS, None, ALU.add))
                step(pool.tensor_tensor(rs, rs, minus_half[:, 0:rs.shape[1]], ALU.pow))
                pool.tensor_tensor(off, off, rs, ALU.mult).then_inc(done, 1)

            def add_bo(b, par):
                pool.wait_ge(xn_ready, 2 * b + 2)
                pool.tensor_tensor(xn_bo[par][:, :, :], xn[:, :, :], b_o[:, :].unsqueeze(1).to_broadcast([P, T, D]),
                                   ALU.add).then_inc(xnbo_ready, 1)

            def accumulate(b, par, u):
                half, j = divmod(u, NC)
                if j == 0:
                    return
                pool.wait_ge(scaled, UNITS * b + u + 1)
                n = 7 * half + j - 1
                if not (isinstance(b, int) and b == 0 and n == 0):
                    pool.wait_ge(summed, 14 * b + n)
                dst = ctx_n[par][:, 4 * half:4 * half + 4, :]
                pool.tensor_tensor(dst, dst, prod[:, u % 2, :, :], ALU.add).then_inc(summed, 1)

            def low(b, which, half, part=part):
                n = 4 * b + 2 * which + half
                high, lo = part
                pool.wait_ge(qk_high, n + 1)
                cols = slice(half * NQ, (half + 1) * NQ)
                pool.tensor_tensor(lo[:, cols], full[:, half, :], high[:, cols].bitcast(F32),
                                   ALU.subtract).then_inc(qk_low, 1)

            def res_beta(b):
                pool.wait_ge(res_loaded, 16 * (b + 1))
                step(pool.tensor_tensor(x_res[:, :, :], x_res[:, :, :], beta[:, :].unsqueeze(1).to_broadcast([P, T, D]),
                                        ALU.add))

            def second_norm(b, half):
                t = slice(4 * half, 4 * half + 4)
                pool.wait_ge(tn_ready, 2 * b + half + 1)
                step(pool.tensor_tensor(g[:, t, :], g[:, t, :], gamma[:, :].unsqueeze(1).to_broadcast([P, 4, D]),
                                        ALU.mult))
                pool.tensor_tensor(g[:, t, :], g[:, t, :], x_res[:, t, :], ALU.add).then_inc(x2_ready, 1)

            def list_entries(b, par, n):
                t, k = divmod(n, 2)
                if n == 0:
                    if isinstance(b, int) and b == 0:
                        pool.wait_ge(lists_blank, 16)
                    wait_apart(pool, listing_ready, b + 1)
                    wait_apart(pool, slots_ready, b + 1)
                pool.indirect_dma_start(out=list_dram[:, :],
                                        out_offset=bass.IndirectOffsetOnAxis(ap=slot[par][:, t, k:k + 1], axis=0),
                                        in_=listing[par][:, t, k, :], in_offset=None,
                                        bounds_check=LIST_TILES * P - 1, oob_is_err=False).then_inc(listed[par], 16)

            def all_listed(b, par, times):
                if isinstance(b, int):
                    pool.wait_ge(listing_free, b + 2)
                    pool.wait_ge(listed[par], 256 * times)
                else:
                    wait_apart(pool, listed[par], 256 * times)
                pool.memset(mark[:, par:par + 1], 0.0).then_inc(listing_free, 1)

            def body(b, par, first=False, last=False, tail=False):
                for s in range(UNITS):
                    if not last and not tail and s == 1:
                        rstd(rs_x[:, :], off_x[:, :], mv_x, stats_x, rstd_x, b + 2)
                    if not first:
                        for half, at in enumerate((2, 10)):
                            t = slice(4 * half, 4 * half + 4)
                            if s == at + 1:
                                rstd(rs_g[:, t], off_g[:, t], mv_g[:, t, :], stats_g, rstd_g, 2 * (b - 1) + half + 1)
                            if s == at + 2:
                                second_norm(b - 1, half)
                        if s == 1:
                            res_beta(b - 1)
                    if lagged(b, s, 8, first, tail):
                        accumulate(before(b, s, 8)[0], par if s >= 8 else 1 - par, before(b, s, 8)[1])
                    if not first:
                        for half, at in enumerate((2, 10)):
                            t = slice(4 * half, 4 * half + 4)
                            if s == at + 3:
                                rstd(rs_y[:, t], off_y[:, t], mv_y[:, t, :], stats_y, rstd_y, 2 * (b - 1) + half + 1)
                    if not last and not tail:
                        if s == 10:
                            if not first:
                                pool.wait_ge(wo_taken, 2 * b)
                            add_bo(b + 1, 1 - par)
                        if s - 1 in PIECES and PIECES[s - 1][0] in ("q", "k"):
                            kind, half = PIECES[s - 1]
                            low(b + 1, int(kind == "k"), half)
                    if has(b, 2):
                        if s in LISTING:
                            list_entries(b - 2, par, 2 * LISTING.index(s))
                            list_entries(b - 2, par, 2 * LISTING.index(s) + 1)
                        if s == UNITS - 1:
                            all_listed(b - 2, par, turn(b, par))

            pool.wait_ge(const_in, CONSTS * 16)
            for par in range(2):
                pool.memset(mark[:, par:par + 1], 0.0).then_inc(listing_free, 1)
            step(pool.memset(minus_half[:, :], -0.5))
            rstd(rs_x[:, :], off_x[:, :], mv_x, stats_x, rstd_x, 1)
            add_bo(0, 0)
            for which in range(2):
                for half in range(2):
                    low(0, which, half, k_part0 if which else part)
            stack(pool, 0, 1, 0, (2, 3), first_low)
            bodies(pool, body, chained, POOL_STEPS)
            for n in range(0, 2 * T, 2):
                list_entries(B - 1, 1, n)
            pool.wait_ge(listed[0], 256 * (B // 2))
            pool.wait_ge(listed[1], 256 * (B // 2) - 128)


DVE_STEPS = 2 * 13
POOL_STEPS = 2 * 13


def expert_phase(nc, a, xy_dram, list_dram, expert_of, list_tile, ident, shared, weights, w_in, out):
    with ExitStack() as ctx:
        def sb(name, shape, dt=F32):
            return ctx.enter_context(nc.sbuf_tensor(name, shape, dt))

        def pb(name):
            return ctx.enter_context(nc.psum_tensor(name, [P, HID], F32))

        def sem(name):
            return ctx.enter_context(nc.semaphore(name))

        w1, w2, b1, b2 = (dst for g in ("probs", "cap", "input") for dst, _ in weights[g])
        entry = sb("entry", [P, RG, 2])
        rows = sb("rows", [P, RG, 2, D])
        xT = sb("xT", [P, 2, P])
        hid = sb("hid", [P, 2, HID])
        hidT = sb("hidT", [P, 2, HB, P])
        y = sb("y", [P, D])
        ps_x, ps_h, ps_t, ps_y = ([pb(f"{n}{i}") for i in range(2)] for n in ("ps_xT", "ps_h", "ps_hT", "ps_y"))

        cleared = sem("cleared")
        last_listed = sem("last_listed")
        entry_in = [sem(f"entry_in{r}") for r in range(RG)]
        gathered = [sem(f"gathered{r}") for r in range(RG)]
        scattered = [sem(f"scattered{r}") for r in range(RG)]
        xT_ready, xT_taken, h_ready, biased = sem("xT_ready_e"), sem("xT_taken_e"), sem("h_ready"), sem("biased")
        gelu_done, hT_ready, hT_taken = sem("gelu_done"), sem("hT_ready"), sem("hT_taken")
        y_ready, y_taken, mixed = sem("y_ready"), sem("y_taken"), sem("mixed")
        block = ctx.enter_context(nc.Block())

        entries = list_dram.rearrange("(n p) c -> n p c", p=P)
        TURNS, PASS_TURNS = NT // RG, TP // RG

        @block.sync
        def _(sp):
            def load(turn, r, first):
                at = sp.value_load(list_tile[0:1, bass.ds(RG * turn + r, 1)], min_val=0, max_val=LIST_TILES - 1)
                if not first:
                    count = sp.snap(16 * turn)
                    sp.compute_val(count)
                    sp.wait_ge(entry_in[r], 16)
                    sp.wait_ge(scattered[r], count)
                sp.dma_start(entry[:, r, :], entries[bass.ds(at, 1), :, :].rearrange("o p c -> (o p) c"))\
                    .then_inc(entry_in[r], 16)

            for r in range(RG):
                load(0, r, True)
            with sp.Fori(1, PASS_TURNS) as i:
                for r in range(RG):
                    load(i, r, False)
            sp.wait_ge(last_listed, 16 * T)
            with sp.Fori(PASS_TURNS, TURNS) as i:
                for r in range(RG):
                    load(i, r, False)

        @block.gpsimd
        def _(pool):
            token = [entry[:, r, 0:1].bitcast(I32) for r in range(RG)]

            def wait_apart(s, count):
                if not isinstance(count, int):
                    count = pool.snap(count)
                    pool.compute_val(count)
                pool.wait_ge(cleared, 1)
                pool.wait_ge(s, count)

            def gather(k, turn, r):
                wait_apart(entry_in[r], 16 * turn + 16)
                pool.indirect_dma_start(out=rows[:, r, :, :].rearrange("p c d -> p (c d)"), out_offset=None,
                                        in_=xy_dram[k][:, :], in_offset=bass.IndirectOffsetOnAxis(ap=token[r], axis=0),
                                        bounds_check=B * N - 1, oob_is_err=False).then_inc(gathered[r], 16)

            def scatter(k, turn, r):
                wait_apart(mixed, RG * turn + r + 1)
                if k == 0:
                    src, dst = rows[:, r, :, :].rearrange("p c d -> p (c d)"), xy_dram[1][:, :]
                else:
                    src, dst = rows[:, r, 1, :], out.rearrange("b n d -> (b n) d")
                pool.indirect_dma_start(out=dst, out_offset=bass.IndirectOffsetOnAxis(ap=token[r], axis=0),
                                        in_=src, in_offset=None,
                                        bounds_check=B * N - 1, oob_is_err=False).then_inc(scattered[r], 16)

            pool.wait_ge(cleared, 1)
            for k in range(2):
                t0 = k * PASS_TURNS
                if k:
                    for r in range(RG):
                        pool.wait_ge(scattered[r], 16 * t0)
                for r in range(AHEAD):
                    if r == RG // 2:
                        pool.wait_ge(cleared, 2)
                    gather(k, t0, r)
                if k == 0:
                    for t in range(T):
                        pool.indirect_dma_start(out=list_dram[:, :],
                                                out_offset=bass.IndirectOffsetOnAxis(ap=shared["slot1"][:, t, 1:2], axis=0),
                                                in_=shared["listing1"][:, t, 1, :], in_offset=None,
                                                bounds_check=LIST_TILES * P - 1, oob_is_err=False)\
                            .then_inc(last_listed, 16)
                with pool.Fori(t0, t0 + PASS_TURNS - 1) as i:
                    for r in range(RG):
                        gather(k, i + (r + AHEAD) // RG, (r + AHEAD) % RG)
                        scatter(k, i, r)
                for r in range(RG):
                    if r + AHEAD < RG:
                        gather(k, t0 + PASS_TURNS - 1, r + AHEAD)
                    scatter(k, t0 + PASS_TURNS - 1, r)
            for r in range(RG):
                pool.wait_ge(scattered[r], 16 * TURNS)

        @block.tensor
        def _(pe):
            def expert_at(n):
                return pe.value_load(expert_of[0:1, bass.ds(n, 1)], min_val=0, max_val=EX - 1)

            def turn_x(turn, r, n):
                pe.wait_ge(gathered[r], 16 * turn + 16)
                if not isinstance(n, int) or n >= 2:
                    pe.wait_ge(xT_taken, n - 1)
                pe.transpose(ps_x[r % 2][:, 0:P], rows[:, r, 0, :], ident[:, :]).then_inc(xT_ready, 1)

            def up(r, n, e):
                pe.wait_ge(xT_taken, n + 1)
                if not isinstance(n, int) or n >= 2:
                    pe.wait_ge(biased, n - 1)
                pe.matmul(ps_h[r % 2][:, :], xT[:, r % 2, :], w1[:, bass.ds(e, 1), :],
                          start=True, stop=True).then_inc(h_ready, 1)

            def turn_h(r, n):
                pe.wait_ge(gelu_done, n + 1)
                if not isinstance(n, int) or n >= 2:
                    pe.wait_ge(hT_taken, n - 1)
                for m in range(HB):
                    last = pe.transpose(ps_t[r % 2][:, m * P:(m + 1) * P], hid[:, r % 2, m * P:(m + 1) * P], ident[:, :])
                last.then_inc(hT_ready, 1)

            def down(r, n, e):
                pe.wait_ge(hT_taken, n + 1)
                if not isinstance(n, int) or n >= 2:
                    pe.wait_ge(y_taken, n - 1)
                for m in range(HB):
                    last = pe.matmul(ps_y[r % 2][:, 0:D], hidT[:, r % 2, m, :], w2[:, bass.ds(e, 1), m, :],
                                     start=(m == 0), stop=(m == HB - 1))
                last.then_inc(y_ready, 1)

            def turn_of(turn, first=False, last=False):
                e = {} if first else {-1: expert_at(RG * turn - 1)}
                e |= {0: expert_at(RG * turn), 1: expert_at(RG * turn + 1)}
                for r in range(RG):
                    n = RG * turn + r
                    if not (last and r + 2 >= RG):
                        turn_x(turn + (r + 2) // RG, (r + 2) % RG, n + 2)
                    if not (last and r + 1 >= RG):
                        up((r + 1) % RG, n + 1, e[r + 1])
                    if r + 2 <= RG and not (last and r + 2 >= RG):
                        e[r + 2] = expert_at(n + 2)
                    turn_h(r, n)
                    if not (first and r == 0):
                        down((r - 1) % RG, n - 1, e[r - 1])

            pe.wait_ge(w_in, sum(len(weights[g]) for g in ("probs", "cap", "input")) * 16)
            for t0 in (0, PASS_TURNS):
                turn_x(t0, 0, RG * t0)
                turn_x(t0, 1, RG * t0 + 1)
                up(0, RG * t0, expert_at(RG * t0))
                turn_of(t0, first=True)
                with pe.Fori(t0 + 1, t0 + PASS_TURNS - 1) as i:
                    turn_of(i)
                turn_of(t0 + PASS_TURNS - 1, last=True)
                down(RG - 1, RG * (t0 + PASS_TURNS) - 1, expert_at(RG * (t0 + PASS_TURNS) - 1))

        @block.scalar
        def _(act):
            def take_x(r, n):
                act.wait_ge(xT_ready, n + 1)
                if not isinstance(n, int) or n >= 2:
                    act.wait_ge(h_ready, n - 1)
                act.activation(xT[:, r % 2, :], ps_x[r % 2][:, 0:P], ACT.Copy).then_inc(xT_taken, 1)

            def gelu(r, n):
                act.wait_ge(biased, n + 1)
                act.activation(hid[:, r % 2, :], hid[:, r % 2, :], ACT.Gelu).then_inc(gelu_done, 1)

            def take_h(r, n):
                act.wait_ge(hT_ready, n + 1)
                if not isinstance(n, int) or n >= 2:
                    act.wait_ge(y_ready, n - 1)
                act.activation(hidT[:, r % 2, :, :], ps_t[r % 2][:, :].rearrange("p (m t) -> p m t", m=HB),
                               ACT.Copy).then_inc(hT_taken, 1)

            def turn_of(turn, last=False):
                for r in range(RG):
                    n = RG * turn + r
                    gelu(r, n)
                    if not (last and r + 2 >= RG):
                        take_x((r + 2) % RG, n + 2)
                    take_h(r, n)

            for t0 in (0, PASS_TURNS):
                take_x(0, RG * t0)
                take_x(1, RG * t0 + 1)
                turn_of(t0)
                with act.Fori(t0 + 1, t0 + PASS_TURNS - 1) as i:
                    turn_of(i)
                turn_of(t0 + PASS_TURNS - 1, last=True)

        @block.vector
        def _(dve):
            for part in range(2):
                dve.memset(rows[:, part * RG // 2:(part + 1) * RG // 2, :, :], 0.0).then_inc(cleared, 1)
            dve.wait_ge(w_in, sum(len(weights[g]) for g in ("probs", "cap", "input")) * 16)

            def expert_at(n):
                return dve.value_load(expert_of[0:1, bass.ds(n, 1)], min_val=0, max_val=EX - 1)

            def bias(r, n):
                e = expert_at(n)
                dve.wait_ge(h_ready, n + 1)
                if not isinstance(n, int) or n >= 2:
                    dve.wait_ge(hT_ready, n - 1)
                dve.tensor_tensor(hid[:, r % 2, :], ps_h[r % 2][:, :],
                                  b1[:, bass.ds(e, 1), :].rearrange("p o h -> p (o h)"), ALU.add).then_inc(biased, 1)

            def mix(r, n):
                e = expert_at(n)
                dve.wait_ge(y_ready, n + 1)
                if not isinstance(n, int) or n >= 1:
                    dve.wait_ge(mixed, n)
                dve.tensor_tensor(y[:, :], ps_y[r % 2][:, 0:D],
                                  b2[:, bass.ds(e, 1), :].rearrange("p o h -> p (o h)"), ALU.add).then_inc(y_taken, 1)
                dve.wait_ge(y_taken, n + 1)
                dve.scalar_tensor_tensor(out=rows[:, r, 1, :], in0=y[:, :], scalar=entry[:, r, 1:2],
                                         in1=rows[:, r, 1, :], op0=ALU.mult, op1=ALU.add).then_inc(mixed, 1)

            def turn_of(turn, first=False, last=False):
                for r in range(RG):
                    n = RG * turn + r
                    if not (last and r + 1 >= RG):
                        bias((r + 1) % RG, n + 1)
                    if not (first and r == 0):
                        mix((r - 1) % RG, n - 1)

            for t0 in (0, PASS_TURNS):
                bias(0, RG * t0)
                turn_of(t0, first=True)
                with dve.Fori(t0 + 1, t0 + PASS_TURNS - 1) as i:
                    turn_of(i)
                turn_of(t0 + PASS_TURNS - 1, last=True)
                mix(RG - 1, RG * (t0 + PASS_TURNS) - 1)


def build(nc, a, out):
    xy_dram = [nc.dram_tensor(f"xy_scratch{k}", [B * N, 2 * D], F32).ap() for k in range(2)]
    list_dram = nc.dram_tensor("list_scratch", [LIST_TILES * P, 2], F32).ap()
    with ExitStack() as ctx:
        ident = ctx.enter_context(nc.sbuf_tensor("ident", [P, P], F32))
        w_in = ctx.enter_context(nc.semaphore("w_in"))
        shared = {name: ctx.enter_context(nc.sbuf_tensor(name, shape, dt)) for name, shape, dt in (
            ("probs", [P, RING, H, NQ], F32), ("cap", [P, NC, N], BF16), ("x_in", [P, T, D], F32),
            ("full", [P, 2, NQ], F32), ("listing1", [P, T, 2, 2], F32), ("slot1", [P, T, 2], I32))}
        w = shared["probs"][:, :, :, :].rearrange("p r h n -> p (r h n)")
        small = shared["full"][:, :, :].rearrange("p h n -> p (h n)")
        expert_of, list_tile = (small[:, 3 * TP + n * NT:3 * TP + (n + 1) * NT].bitcast(I32) for n in range(2))
        weights = {
            "probs": [(w[:, 0:EX * HID].rearrange("p (e h) -> p e h", e=EX), "W1"),
                      (w[:, EX * HID:].rearrange("p (e m d) -> p e m d", e=EX, m=HB), "W2")],
            "cap": [(shared["cap"][:, :, :].rearrange("p j n -> p (j n)").bitcast(F32)
                     .rearrange("p (e h) -> p e h", e=EX), "b1")],
            "input": [(shared["x_in"][:, :, :], "b2")],
            "table": [(small[:, 0:TP], "tile_no"),
                      (small[:, TP:3 * TP].rearrange("p (k t) -> p k t", k=2), "tile_base"),
                      (small[:, NQ:NQ + EX * EX].rearrange("p (e f) -> p e f", e=EX), "lower"),
                      (small[:, NQ + EX * EX:NQ + EX * EX + 2 * EX].rearrange("p (k e) -> p k e", k=2), "slot0")]}
        a = a | {"W1": a["W1"].rearrange("e p h -> p e h"), "W2": a["W2"].rearrange("e (m p) d -> p e m d", p=P)}
        attention_phase(nc, a, xy_dram[0], list_dram, expert_of, list_tile, ident, shared, weights, w_in)
        expert_phase(nc, a, xy_dram, list_dram, expert_of, list_tile, ident, shared, weights, w_in, out)


def kernel(**inputs):
    import numpy as np
    import concourse.bacc as bacc
    from concourse.bass_utils import run_bass_kernel_spmd

    g = {k: np.asarray(v) for k, v in inputs.items()}

    def rows(v):
        return np.ascontiguousarray(np.broadcast_to(v[None], (P,) + v.shape))

    arrays = {
        "x": g["x"], "adjT": np.ascontiguousarray(g["adj"].T),
        "WqT": np.ascontiguousarray(g["L0_gnn_Wq"].T), "WkT": np.ascontiguousarray(g["L0_gnn_Wk"].T),
        "WvT": np.ascontiguousarray(g["L0_gnn_Wv"].T), "WoT": np.ascontiguousarray(g["L0_gnn_Wo"].T),
        "bq": g["L0_gnn_bq"].reshape(P, 1), "bk": g["L0_gnn_bk"].reshape(P, 1),
        "bv": rows(g["L0_gnn_bv"]), "bo": rows(g["L0_gnn_bo"]),
        "gamma": rows(g["L0_gnn_gamma"]), "beta": rows(g["L0_gnn_beta"]),
        "Wg": g["L0_ffn_Wg"], "bg": rows(g["L0_ffn_bg"]),
        "W1": g["L0_ffn_W1"], "W2": g["L0_ffn_W2"],
        "b1": rows(g["L0_ffn_b1"]), "b2": rows(g["L0_ffn_b2"]),
        "ident": np.eye(P, dtype=np.float32), "iota": rows(np.arange(EX, dtype=np.float32)),
    }
    slot0 = np.array([[(k * PASS_TILES + e * CAP // P) * P for e in range(EX)] for k in range(2)], np.float32)
    pads = np.zeros((P, 2), np.float32)
    pads.view(np.int32)[:, 0] = B * N + np.arange(P)
    arrays |= {
        "earlier": np.triu(np.ones((P, P), np.float32), 1),
        "token_no": np.ascontiguousarray(np.arange(B * N, dtype=np.int32).reshape(B * T, P).T),
        "slot0": rows(slot0), "pads": rows(pads.reshape(-1)),
        "lower": rows(np.tril(np.ones((EX, EX), np.float32))), "tile_no": rows(np.arange(TP, dtype=np.float32)),
        "tile_base": rows(np.array([[k * PASS_TILES + i for i in range(TP)] for k in range(2)], np.float32)),
    }
    nc = bacc.Bacc("TRN2", target_bir_lowering=False, num_devices=1)
    a = {k: nc.dram_tensor(k + "_dram", v.shape, mybir.dt.from_np(v.dtype), kind="ExternalInput").ap()
         for k, v in arrays.items()}
    out = nc.dram_tensor("out", (B, N, D), F32, kind="ExternalOutput").ap()
    build(nc, a, out)
    r = run_bass_kernel_spmd(nc, [{k + "_dram": v for k, v in arrays.items()}], core_ids=[0])
    return r.results[0]["out"]
```
